# Optimizing a Trainium2 kernel written in Bass

```python
import numpy as np
import jax
import jax.numpy as jnp

def _softmax(x, axis=-1):
    return jax.nn.softmax(x, axis=axis)

def _gelu(x):
    return jax.nn.gelu(x, approximate=True)

def _silu(x):
    return jax.nn.silu(x)

def _sigmoid(x):
    return jax.nn.sigmoid(x)

def _layernorm(x, axis=-1, eps=1e-05):
    m = jnp.mean(x, axis=axis, keepdims=True)
    v = jnp.var(x, axis=axis, keepdims=True)
    return (x - m) / jnp.sqrt(v + eps)

def _scatter_add(tgt, idx, src, axis=0):
    return tgt.at[idx].add(src)

def _segment_sum(src, seg, n):
    return jax.ops.segment_sum(src, seg, n)
kernel_name = 'mk_xattn_ffn_d2_seqx_r8_a3b73a'

def setup_inputs(seed: int=0):
    np.random.seed(seed)
    _w = jnp.asarray

    def _rec_inputs():
        import jax
        import jax.numpy as jnp
        _rk = jax.random.key(seed)
        x = 7.22e-05 + 1 * jax.random.normal(jax.random.fold_in(_rk, 1), (32, 128, 128), jnp.float32)
        _lenS = 128 - jax.random.randint(jax.random.fold_in(_rk, 7), (32,), 0, max(1, 128 // 4) + 1, jnp.int32)
        _lenS2 = 128 - jax.random.randint(jax.random.fold_in(_rk, 8), (32,), 0, max(1, 128 // 4) + 1, jnp.int32)
        _ctx_1024P = jax.random.normal(jax.random.fold_in(_rk, 11), (32, 16, 128), jnp.float32)
        _ctx_1024c = jax.random.dirichlet(jax.random.fold_in(_rk, 511), 0.3 * jnp.ones((16,), jnp.float32), (32, 128))
        _ctx_1024t = jnp.einsum('bsk,bkd->bsd', _ctx_1024c, _ctx_1024P)
        _ctx_1024t = _ctx_1024t * jax.lax.rsqrt(jnp.mean(jnp.square(_ctx_1024t)) + 1e-12) * 0.953939
        ctx_1024 = 4.13588e-05 + 0.999923 * (_ctx_1024t + 0.3 * jax.random.normal(jax.random.fold_in(_rk, 611), (32, 128, 128), jnp.float32))
        return (x, ctx_1024)
    x, ctx_1024 = _rec_inputs()

    def _L0_xattn_setup():
        import jax, jax.numpy as jnp
        import numpy as np
        WINDOW = 32

        def _band_attention(qh, k, v, w):
            B, H, L, hd = qh.shape
            nb = L // w
            qb = qh.reshape(B, H, nb, w, hd)
            kp = jnp.pad(k, ((0, 0), (w, w), (0, 0))).reshape(B, nb + 2, w, hd)
            vp = jnp.pad(v, ((0, 0), (w, w), (0, 0))).reshape(B, nb + 2, w, hd)
            kwin = jnp.concatenate([kp[:, :-2], kp[:, 1:-1], kp[:, 2:]], axis=2)
            vwin = jnp.concatenate([vp[:, :-2], vp[:, 1:-1], vp[:, 2:]], axis=2)
            scores = jnp.einsum('bhnqd,bnkd->bhnqk', qb, kwin)
            qpos = jnp.arange(w)
            kpos = jnp.arange(3 * w)
            rel = kpos[None, :] - (w + qpos[:, None])
            band = jnp.abs(rel) <= w
            absk = jnp.arange(nb)[:, None, None] * w + kpos[None, None, :] - w
            valid = band[None] & (absk >= 0) & (absk < L)
            neg = jnp.asarray(jnp.finfo(scores.dtype).min, scores.dtype)
            scores = jnp.where(valid[None, None], scores, neg)
            probs = jax.nn.softmax(scores, axis=-1)
            out = jnp.einsum('bhnqk,bnkd->bhnqd', probs, vwin)
            return out.reshape(B, H, L, hd)
        key = jax.random.key(seed)
        kq, kkv, k1, k2, k3 = jax.random.split(key, 5)
        B, L, D, H = (1, 1024, 128, 16)
        hd = D // H
        s = D ** (-0.5)
        return {'q': jax.random.normal(kq, (B, L, D), jnp.float32), 'kv': jax.random.normal(kkv, (B, L, D), jnp.float32), 'w_q': jax.random.normal(k1, (D, D), jnp.float32) * s, 'w_kv': jax.random.normal(k2, (D, 2 * hd), jnp.float32) * s, 'w_o': jax.random.normal(k3, (D, D), jnp.float32) * s}
    _L0_xattn_all = _L0_xattn_setup()
    _L0_xattn_in = {k: v for k, v in _L0_xattn_all.items() if k in ('w_q', 'w_kv', 'w_o')}
    del _L0_xattn_all

    def _L0_ffn_setup():
        import jax, jax.numpy as jnp
        import numpy as np
        D_MODEL = 128
        EXPERT_DIM = 256
        N_EXPERTS = 8
        LN_EPS = 1e-05

        def _bit_quant(W):
            scale = jnp.clip(jnp.mean(jnp.abs(W), axis=-1, keepdims=True), 1e-05, None)
            w_q = jnp.clip(jnp.round(W / scale), -1.0, 1.0) * scale
            return W + jax.lax.stop_gradient(w_q - W)
        key = jax.random.key(seed)
        ks = jax.random.split(key, 7)
        x = jax.random.normal(ks[0], (4, 256, D_MODEL), dtype=jnp.float32)
        shared_w1 = jax.random.normal(ks[1], (EXPERT_DIM, D_MODEL), dtype=jnp.float32) / np.sqrt(EXPERT_DIM)
        shared_w2 = jax.random.normal(ks[2], (D_MODEL, EXPERT_DIM), dtype=jnp.float32) / np.sqrt(D_MODEL)
        expert_w1 = jax.random.normal(ks[3], (N_EXPERTS, EXPERT_DIM, D_MODEL), dtype=jnp.float32) / np.sqrt(EXPERT_DIM)
        expert_w2 = jax.random.normal(ks[4], (N_EXPERTS, D_MODEL, EXPERT_DIM), dtype=jnp.float32) / np.sqrt(D_MODEL)
        router_w = 0.02 * jax.random.normal(ks[5], (N_EXPERTS, D_MODEL), dtype=jnp.float32)
        ln_gamma = jnp.ones((D_MODEL,), dtype=jnp.float32)
        ln_beta = jnp.zeros((D_MODEL,), dtype=jnp.float32)
        return {'x': x, 'shared_w1': shared_w1, 'shared_w2': shared_w2, 'expert_w1': expert_w1, 'expert_w2': expert_w2, 'router_w': router_w, 'ln_gamma': ln_gamma, 'ln_beta': ln_beta}
    _L0_ffn_all = _L0_ffn_setup()
    _L0_ffn_in = {k: v for k, v in _L0_ffn_all.items() if k in ('shared_w1', 'shared_w2', 'expert_w1', 'expert_w2', 'router_w', 'ln_gamma', 'ln_beta')}
    del _L0_ffn_all

    def _L1_xattn_setup():
        import jax, jax.numpy as jnp
        import numpy as np
        D_MODEL = 128
        H = 16
        D_K = D_MODEL // H
        key = jax.random.key(seed)
        ks = jax.random.split(key, 11)
        B, S = (2, 256)
        scale = 1.0 / np.sqrt(D_MODEL)
        inp = {'query': jax.random.normal(ks[0], (B, S, D_MODEL), jnp.float32), 'key': jax.random.normal(ks[1], (B, S, D_MODEL), jnp.float32), 'value': jax.random.normal(ks[2], (B, S, D_MODEL), jnp.float32), 'Wq': jax.random.normal(ks[3], (D_MODEL, D_MODEL), jnp.float32) * scale, 'bq': jnp.zeros((D_MODEL,), jnp.float32), 'Wk': jax.random.normal(ks[4], (D_MODEL, D_MODEL), jnp.float32) * scale, 'bk': jnp.zeros((D_MODEL,), jnp.float32), 'Wv': jax.random.normal(ks[5], (D_MODEL, D_MODEL), jnp.float32) * scale, 'bv': jnp.zeros((D_MODEL,), jnp.float32), 'Wo': jax.random.normal(ks[6], (D_MODEL, D_MODEL), jnp.float32) * scale, 'bo': jnp.zeros((D_MODEL,), jnp.float32)}
        return inp
    _L1_xattn_all = _L1_xattn_setup()
    _L1_xattn_in = {k: v for k, v in _L1_xattn_all.items() if k in ('Wq', 'bq', 'Wk', 'bk', 'Wv', 'bv', 'Wo', 'bo')}
    del _L1_xattn_all

    def _L1_ffn_setup():
        import jax, jax.numpy as jnp
        import numpy as np
        B, S, D_MODEL, D_HIDDEN = (4, 256, 128, 512)

        def act_quant(x):
            scale = 127.0 / jnp.clip(jnp.max(jnp.abs(x), axis=-1, keepdims=True), 1e-05)
            return jnp.clip(jnp.round(x * scale), -128, 127) / scale

        def weight_quant(w):
            scale = 1.0 / jnp.clip(jnp.mean(jnp.abs(w)), 1e-05)
            return jnp.clip(jnp.round(w * scale), -1, 1) / scale

        def bit_linear(x, w):
            xq = x + jax.lax.stop_gradient(act_quant(x) - x)
            wq = w + jax.lax.stop_gradient(weight_quant(w) - w)
            return jnp.einsum('bsd,hd->bsh', xq, wq)

        def depthwise_conv1d(x_bcl, w, b):
            y = jax.lax.conv_general_dilated(x_bcl, w, window_strides=(1,), padding=[(1, 1)], dimension_numbers=('NCH', 'OIH', 'NCH'), feature_group_count=x_bcl.shape[1])
            return y + b[None, :, None]
        key = jax.random.key(seed)
        ks = jax.random.split(key, 5)
        lim1 = 1.0 / np.sqrt(D_MODEL)
        lim2 = 1.0 / np.sqrt(D_HIDDEN)
        limc = 1.0 / np.sqrt(3.0)
        return {'x': jax.random.normal(ks[0], (B, S, D_MODEL), dtype=jnp.float32), 'w1': jax.random.uniform(ks[1], (D_HIDDEN, D_MODEL), jnp.float32, -lim1, lim1), 'conv_w': jax.random.uniform(ks[2], (D_HIDDEN, 1, 3), jnp.float32, -limc, limc), 'conv_b': jax.random.uniform(ks[3], (D_HIDDEN,), jnp.float32, -limc, limc), 'w2': jax.random.uniform(ks[4], (D_MODEL, D_HIDDEN), jnp.float32, -lim2, lim2)}
    _L1_ffn_all = _L1_ffn_setup()
    _L1_ffn_in = {k: v for k, v in _L1_ffn_all.items() if k in ('w1', 'conv_w', 'conv_b', 'w2')}
    del _L1_ffn_all
    return {'x': x, 'ctx_1024': ctx_1024, 'L0_xattn_w_q': _L0_xattn_in['w_q'], 'L0_xattn_w_kv': _L0_xattn_in['w_kv'], 'L0_xattn_w_o': _L0_xattn_in['w_o'], 'L0_ffn_shared_w1': _L0_ffn_in['shared_w1'], 'L0_ffn_shared_w2': _L0_ffn_in['shared_w2'], 'L0_ffn_expert_w1': _L0_ffn_in['expert_w1'], 'L0_ffn_expert_w2': _L0_ffn_in['expert_w2'], 'L0_ffn_router_w': _L0_ffn_in['router_w'], 'L0_ffn_ln_gamma': _L0_ffn_in['ln_gamma'], 'L0_ffn_ln_beta': _L0_ffn_in['ln_beta'], 'L1_xattn_Wq': _L1_xattn_in['Wq'], 'L1_xattn_bq': _L1_xattn_in['bq'], 'L1_xattn_Wk': _L1_xattn_in['Wk'], 'L1_xattn_bk': _L1_xattn_in['bk'], 'L1_xattn_Wv': _L1_xattn_in['Wv'], 'L1_xattn_bv': _L1_xattn_in['bv'], 'L1_xattn_Wo': _L1_xattn_in['Wo'], 'L1_xattn_bo': _L1_xattn_in['bo'], 'L1_ffn_w1': _L1_ffn_in['w1'], 'L1_ffn_conv_w': _L1_ffn_in['conv_w'], 'L1_ffn_conv_b': _L1_ffn_in['conv_b'], 'L1_ffn_w2': _L1_ffn_in['w2']}

def reference(x, ctx_1024, L0_xattn_w_q, L0_xattn_w_kv, L0_xattn_w_o, L0_ffn_shared_w1, L0_ffn_shared_w2, L0_ffn_expert_w1, L0_ffn_expert_w2, L0_ffn_router_w, L0_ffn_ln_gamma, L0_ffn_ln_beta, L1_xattn_Wq, L1_xattn_bq, L1_xattn_Wk, L1_xattn_bk, L1_xattn_Wv, L1_xattn_bv, L1_xattn_Wo, L1_xattn_bo, L1_ffn_w1, L1_ffn_conv_w, L1_ffn_conv_b, L1_ffn_w2):
    import jax
    import jax.numpy as jnp

    def _L0_xattn_ref(q, kv, w_q, w_kv, w_o):
        import jax, jax.numpy as jnp
        import numpy as np
        WINDOW = 32

        def _band_attention(qh, k, v, w):
            B, H, L, hd = qh.shape
            nb = L // w
            qb = qh.reshape(B, H, nb, w, hd)
            kp = jnp.pad(k, ((0, 0), (w, w), (0, 0))).reshape(B, nb + 2, w, hd)
            vp = jnp.pad(v, ((0, 0), (w, w), (0, 0))).reshape(B, nb + 2, w, hd)
            kwin = jnp.concatenate([kp[:, :-2], kp[:, 1:-1], kp[:, 2:]], axis=2)
            vwin = jnp.concatenate([vp[:, :-2], vp[:, 1:-1], vp[:, 2:]], axis=2)
            scores = jnp.einsum('bhnqd,bnkd->bhnqk', qb, kwin)
            qpos = jnp.arange(w)
            kpos = jnp.arange(3 * w)
            rel = kpos[None, :] - (w + qpos[:, None])
            band = jnp.abs(rel) <= w
            absk = jnp.arange(nb)[:, None, None] * w + kpos[None, None, :] - w
            valid = band[None] & (absk >= 0) & (absk < L)
            neg = jnp.asarray(jnp.finfo(scores.dtype).min, scores.dtype)
            scores = jnp.where(valid[None, None], scores, neg)
            probs = jax.nn.softmax(scores, axis=-1)
            out = jnp.einsum('bhnqk,bnkd->bhnqd', probs, vwin)
            return out.reshape(B, H, L, hd)
        B, L, D = q.shape
        hd = w_kv.shape[-1] // 2
        H = D // hd
        qh = (q @ w_q).reshape(B, L, H, hd).transpose(0, 2, 1, 3)
        k, v = jnp.split(kv @ w_kv, 2, axis=-1)
        o = _band_attention(qh, k, v, WINDOW)
        o = o.transpose(0, 2, 1, 3).reshape(B, L, D)
        return o @ w_o

    def _L0_ffn_ref(x, shared_w1, shared_w2, expert_w1, expert_w2, router_w, ln_gamma, ln_beta):
        import jax, jax.numpy as jnp
        import numpy as np
        D_MODEL = 128
        EXPERT_DIM = 256
        N_EXPERTS = 8
        LN_EPS = 1e-05

        def _bit_quant(W):
            scale = jnp.clip(jnp.mean(jnp.abs(W), axis=-1, keepdims=True), 1e-05, None)
            w_q = jnp.clip(jnp.round(W / scale), -1.0, 1.0) * scale
            return W + jax.lax.stop_gradient(w_q - W)
        mu = jnp.mean(x, axis=-1, keepdims=True)
        var = jnp.mean(jnp.square(x - mu), axis=-1, keepdims=True)
        h = (x - mu) / jnp.sqrt(var + LN_EPS) * ln_gamma + ln_beta
        sw1, sw2 = (_bit_quant(shared_w1), _bit_quant(shared_w2))
        shared_out = jax.nn.silu(jnp.einsum('btd,fd->btf', h, sw1)) @ sw2.T
        probs = jax.nn.softmax(h @ router_w.T, axis=-1)
        top_prob = jnp.max(probs, axis=-1)
        top_idx = jnp.argmax(probs, axis=-1)
        ew1, ew2 = (_bit_quant(expert_w1), _bit_quant(expert_w2))
        h1 = jax.nn.silu(jnp.einsum('btd,efd->ebtf', h, ew1))
        eo = jnp.einsum('ebtf,edf->ebtd', h1, ew2)
        gate = jax.nn.one_hot(top_idx, N_EXPERTS, dtype=h.dtype) * top_prob[..., None]
        routed_out = jnp.einsum('ebtd,bte->btd', eo, gate)
        return shared_out + routed_out

    def _L1_xattn_ref(query, key, value, Wq, bq, Wk, bk, Wv, bv, Wo, bo):
        import jax, jax.numpy as jnp
        import numpy as np
        D_MODEL = 128
        H = 16
        D_K = D_MODEL // H
        B, Sq, _ = query.shape

        def proj(x, W, b):
            y = x @ W.T + b
            return y.reshape(B, -1, H, D_K).transpose(0, 2, 1, 3)
        q = proj(query, Wq, bq)
        k = proj(key, Wk, bk)
        v = proj(value, Wv, bv)
        scores = jnp.einsum('bhqd,bhkd->bhqk', q, k) / jnp.sqrt(jnp.float32(D_K))
        attn = jax.nn.softmax(scores, axis=-1)
        ctx = jnp.einsum('bhqk,bhkd->bhqd', attn, v)
        ctx = ctx.transpose(0, 2, 1, 3).reshape(B, Sq, D_MODEL)
        return ctx @ Wo.T + bo

    def _L1_ffn_ref(x, w1, conv_w, conv_b, w2):
        import jax, jax.numpy as jnp
        import numpy as np
        B, S, D_MODEL, D_HIDDEN = (4, 256, 128, 512)

        def act_quant(x):
            scale = 127.0 / jnp.clip(jnp.max(jnp.abs(x), axis=-1, keepdims=True), 1e-05)
            return jnp.clip(jnp.round(x * scale), -128, 127) / scale

        def weight_quant(w):
            scale = 1.0 / jnp.clip(jnp.mean(jnp.abs(w)), 1e-05)
            return jnp.clip(jnp.round(w * scale), -1, 1) / scale

        def bit_linear(x, w):
            xq = x + jax.lax.stop_gradient(act_quant(x) - x)
            wq = w + jax.lax.stop_gradient(weight_quant(w) - w)
            return jnp.einsum('bsd,hd->bsh', xq, wq)

        def depthwise_conv1d(x_bcl, w, b):
            y = jax.lax.conv_general_dilated(x_bcl, w, window_strides=(1,), padding=[(1, 1)], dimension_numbers=('NCH', 'OIH', 'NCH'), feature_group_count=x_bcl.shape[1])
            return y + b[None, :, None]
        h = bit_linear(x, w1)
        h = depthwise_conv1d(h.transpose(0, 2, 1), conv_w, conv_b)
        h = h.transpose(0, 2, 1)
        h = jax.nn.silu(h)
        return bit_linear(h, w2)
    x = x + _L0_xattn_ref(_layernorm(x, axis=-1), ctx_1024, L0_xattn_w_q, L0_xattn_w_kv, L0_xattn_w_o)
    x = x + _L0_ffn_ref(_layernorm(x, axis=-1), L0_ffn_shared_w1, L0_ffn_shared_w2, L0_ffn_expert_w1, L0_ffn_expert_w2, L0_ffn_router_w, L0_ffn_ln_gamma, L0_ffn_ln_beta)
    x = x + _L1_xattn_ref(_layernorm(x, axis=-1), ctx_1024, ctx_1024, L1_xattn_Wq, L1_xattn_bq, L1_xattn_Wk, L1_xattn_bk, L1_xattn_Wv, L1_xattn_bv, L1_xattn_Wo, L1_xattn_bo)
    x = x + _L1_ffn_ref(_layernorm(x, axis=-1), L1_ffn_w1, L1_ffn_conv_w, L1_ffn_conv_b, L1_ffn_w2)
    return x

_drawn_inputs = setup_inputs


def setup_inputs(seed=0):
    import zlib

    import numpy as np

    out = dict(_drawn_inputs(seed))
    spreads = {'L0_ffn_ln_gamma': (1.0, 0.2),
     'L0_ffn_ln_beta': (0.0, 0.39),
     'L1_xattn_bq': (0.0, 0.501),
     'L1_xattn_bk': (0.0, 0.8),
     'L1_xattn_bv': (0.0, 0.1),
     'L1_xattn_bo': (0.0, 0.1)}
    factors = {}
    for name, (base, spread) in spreads.items():
        noise = np.random.default_rng([zlib.crc32(name.encode()), seed]).standard_normal(out[name].shape)
        drawn = base * np.exp(spread * noise) if base else spread * noise
        out[name] = jnp.asarray(drawn.astype(out[name].dtype))
    for name, factor in factors.items():
        out[name] = (out[name] * factor).astype(out[name].dtype)
    return out
```

```python
from contextlib import ExitStack

import concourse.bass as bass
from concourse import mybir

F32 = mybir.dt.float32
F16 = mybir.dt.float16
ALU = mybir.AluOpType
ACT = mybir.ActivationFunctionType
AX = mybir.AxisListType

P = 128
B = 32
S = 128
D = 128
H = 16
DH = D // H
GB = 4
NG = B // GB
GT = GB * S
WINDOW = 32
E = 8
EF = 256
FB = EF // P
CF = 512
CB = CF // P
EPS = 1e-5
SPLIT = 64.0
S2 = SPLIT * SPLIT
MASK = 60000.0
NM = P - 1
TERMS = 4
UP, LOW = TERMS * DH, 96
ROUND = 12582912.0
VW = DH + 1

W1E, W1S, W2E, W2S, W1C, W2C = 0, E * FB, (E + 1) * FB, (2 * E + 1) * FB, 2 * (E + 1) * FB, 2 * (E + 1) * FB + CB
NW = W2C + CB


class At:

    def __init__(self, i, off, span, size):
        self.i, self.off, self.span, self.size = i, off, span, size

    def back(self, lag):
        return At(self.i, self.off - lag, self.span, self.size)

    def live(self):
        return not isinstance(self.i, int) or 0 <= self.span * self.i + self.off < self.size

    def count(self, per, extra=0):
        value = self.i * (self.span * per) + (self.off * per + extra)
        return max(value, 0) if isinstance(value, int) else value

    def group(self):
        return At(self.i, self.off // GB, self.span // GB, self.size // GB)

    def arrivals(self, per):
        return self.i * (self.span // 2 * per) + (self.off // 2 + 1) * per

    @property
    def slot(self):
        return self.off % 2


def pipeline(eng, span, size, lag, step):
    assert lag <= span and size % span == 0
    for j in range(span):
        step(At(0, j, span, size))
    with eng.Fori(1, size // span) as i:
        for j in range(span):
            step(At(i, j, span, size))
    for j in range(lag):
        step(At(size // span, j, span, size))


class Memory:
    pass


class Chain:

    def __init__(self, eng, sem, strict=False):
        self.eng, self.sem, self.strict, self.n = eng, sem, strict, 0

    def then(self, ins):
        self.n += 1
        ins.then_inc(self.sem, 1)
        if self.strict:
            self.last()

    def last(self):
        self.eng.wait_ge(self.sem, self.n)


def setup(nc, m, a, sem):
    small_in = sem("small_weights_loaded")
    ffn_in = sem("ffn_weights_loaded")
    pool_made = sem("pool_constants")
    dve_made = sem("dve_setup_steps")
    act_made = sem("act_setup_steps")
    ternary = sem("ternary_ready")
    transposed = sem("weights_transposed")
    kept = sem("transposed_weights_kept")
    projected = sem("constants_projected")
    with nc.sbuf_tensor("w_nat", [P, NW, P], F32) as w_nat, nc.sbuf_tensor("tern", [P, NW, P], F16) as tern, \
            nc.sbuf_tensor("abs_sum", [P, NW], F32) as abs_sum, nc.sbuf_tensor("inv", [P, NW], F32) as inv, \
            nc.sbuf_tensor("scale_rows", [P, 3, 16], F32) as scale_rows, \
            nc.sbuf_tensor("part_sums", [P, 2], F32) as part_sums, nc.Block() as block:
        small = [(m.wq[0], a["wq0"]), (m.wk[0], a["wk0"]), (m.wv[0], a["wv0"]), (m.wo[0], a["wo0"]), (m.wq[1], a["wq1"]),
                 (m.wk[1], a["wk1"]), (m.wv[1], a["wv1"]), (m.wo[1], a["wo1"]), (m.rw, a["rw"]),
                 (m.qkb, a["bqk"]), (m.bv, a["bv"]), (m.cw, a["cw"]), (m.cb, a["cb"])]
        rows = [(m.gamma, a["gamma"]), (m.beta, a["beta"]), (m.bo, a["bo"])]

        @block.sync
        def _(sp):
            big = [(w_nat[:, W1E:W1S, :], a["w1e"].rearrange("e (f p) d -> p (e f) d", p=P)),
                   (w_nat[:, W1S:W2E, :], a["w1s"].rearrange("(f p) d -> p f d", p=P)),
                   (w_nat[:, W2E:W2S, :].rearrange("p (e f) d -> p e (f d)", e=E), a["w2e"].rearrange("e p f -> p e f")),
                   (w_nat[:, W2S:W1C, :].rearrange("p f d -> p (f d)"), a["w2s"]),
                   (w_nat[:, W1C:W2C, :], a["w1c"].rearrange("(f p) d -> p f d", p=P)),
                   (w_nat[:, W2C:NW, :].rearrange("p f d -> p (f d)"), a["w2c"])]
            for dst, src in big:
                sp.dma_start(dst, src).then_inc(ffn_in, 16)
            for g in range(NG):
                sp.dma_start(m.x[:, GB * g:GB * g + GB, :],
                             a["x"][GB * g:GB * g + GB].rearrange("b p d -> p b d")).then_inc(m.x_in, 16)

        @block.scalar
        def _(act):
            for dst, src in small:
                act.dma_start(dst[tuple(slice(None) for _ in dst.shape)], src).then_inc(small_in, 16)
            for dst, src in rows:
                act.dma_start(dst[:, :], src.to_broadcast([P, D])).then_inc(small_in, 16)
            for k in range(NW // 4):
                act.wait_ge(transposed, k + 1)
                nc.scalar.activation(m.w_t[:, 4 * k:4 * k + 4, :].rearrange("p w d -> p (w d)"),
                                     m.bank[k % 2][:, 0:256].bitcast(F16), ACT.Copy).then_inc(kept, 1)
            act.wait_ge(projected, 2)
            act.wait_ge(dve_made, 1)
            nc.scalar.activation(m.s1_t[0:16, :, :].rearrange("p f d -> p (f d)"), m.bank[3][0:16, 0:256], ACT.Copy,
                                 scale=0.5).then_inc(act_made, 1)
            nc.scalar.activation(m.s2_t[0:16, :], m.bank[3][0:16, 256:384], ACT.Copy, scale=1.0 / SPLIT).then_inc(act_made, 1)

        @block.gpsimd
        def _(pl):
            g = nc.gpsimd
            step = Chain(pl, pool_made, strict=True)
            step.then(g.memset(m.id32[:, :], 0.0))
            step.then(g.memset(m.id16[:, :], 0.0))
            for t in (m.id32, m.id16):
                step.then(g.affine_select(out=t[:, :], in_=t[:, :], compare_op=ALU.not_equal, fill=1.0, base=0,
                                          pattern=[[-1, P]], channel_multiplier=1))
            for t, value in ((m.minus_half, -0.5), (m.quarter, D / 4), (m.per_d, 1.0 / D), (m.eps, EPS)):
                step.then(g.memset(t[:, :], value))
            step.then(g.memset(m.ones[:, :], 1.0))
            step.then(g.memset(m.pick[:, :, :], 0.0))
            for e in range(E):
                step.then(g.memset(m.rank[:, e:e + 1], float(E - e)))
            step.then(g.memset(m.band_q[:, :, :], MASK))
            step.then(g.memset(m.band_k[:, :, :], -MASK))
            step.then(g.memset(m.plain_k[:, :], 0.0))
            step.then(g.affine_select(out=m.pick[:, :, :], in_=m.pick[:, :, :], compare_op=ALU.not_equal, fill=1.0,
                                      base=0, pattern=[[-1, E], [0, P]], channel_multiplier=1))
            for half in range(2):
                q0, dq, k0, dk = (0, 1, 0, 1) if half == 0 else (63, -1, S - 1, -1)
                for lo_p, hi_p, tile, base, step_x, mult in (
                        (0, LOW, m.band_q, -UP - q0, -dq, 1), (0, LOW, m.band_k, k0 + UP - WINDOW - 1, dk, -1),
                        (LOW, P, m.band_q, q0 - WINDOW - 1, dq, -1), (LOW, P, m.band_k, -k0, -dk, 1)):
                    part = tile[lo_p:hi_p, half, :]
                    step.then(g.affine_select(out=part, in_=part, compare_op=ALU.is_ge, fill=0.0, base=base,
                                              pattern=[[step_x, part.shape[-1]]], channel_multiplier=mult))
            for tile, fill, first in ((m.band_q, 0.0, LOW), (m.band_k, S2, LOW), (m.plain_k, S2, 0)):
                part = tile[first:P]
                part = part.rearrange("p a b -> p (a b)") if len(tile.shape) == 3 else part
                step.then(g.affine_select(out=part, in_=part, compare_op=ALU.is_gt, fill=fill, base=NM - first,
                                          pattern=[[0, part.shape[-1]]], channel_multiplier=-1))

        @block.vector
        def _(dve):
            v = nc.vector
            step = Chain(dve, dve_made)
            for t in (m.s1_t, m.s2_t, m.o_t32, m.o_t16, scale_rows):
                last = v.memset(t[tuple(slice(None) for _ in t.shape)], 0.0)
            step.then(last)
            dve.wait_ge(ffn_in, 6 * 16)
            step.last()
            step.then(v.tensor_reduce(abs_sum[:, :], w_nat[:, :, :], AX.X, ALU.add, apply_absolute_value=True))
            step.last()
            step.then(v.tensor_scalar(m.s1[:, :], abs_sum[:, W1E:W2E], 1.0 / D, EPS, ALU.mult, ALU.max))
            pairs = abs_sum[:, W2E:W1C].rearrange("p (e f) -> p f e", f=FB)
            step.then(v.tensor_tensor(m.s2[:, :], pairs[:, 0, :], pairs[:, 1, :], ALU.add))
            for k, at in enumerate((W1C, W2C)):
                step.then(v.tensor_reduce(part_sums[:, k:k + 1], abs_sum[:, at:at + CB], AX.X, ALU.add))
            step.last()
            sums_ready = step.n
            step.then(v.tensor_scalar(m.s2[:, :], m.s2[:, :], 1.0 / EF, EPS, ALU.mult, ALU.max))
            step.last()
            step.then(v.reciprocal(inv[:, W1E:W2E], m.s1[:, :]))
            step.then(v.reciprocal(inv[:, W2E:W1C:2], m.s2[:, :]))
            step.then(v.reciprocal(inv[:, W2E + 1:W1C:2], m.s2[:, :]))
            step.then(v.tensor_copy(scale_rows[:, 0:FB, 0:E], m.s1[:, 0:E * FB].rearrange("p (e f) -> p f e", f=FB)))
            step.then(v.tensor_copy(scale_rows[:, FB, E:2 * E], m.s2[:, 0:E]))
            assert sums_ready == 6 and step.n == 12
            dve.wait_ge(projected, 1)
            step.then(v.tensor_scalar(m.sc[:, :], m.bank[2][:, 0:2], 1.0 / (CF * D), EPS, ALU.mult, ALU.max))
            step.last()
            step.then(v.reciprocal(part_sums[:, :], m.sc[:, :]))
            step.last()
            for k, at in enumerate((W1C, W2C)):
                step.then(v.tensor_copy(inv[:, at:at + CB], part_sums[:, k:k + 1].to_broadcast([P, CB])))
            step.last()
            for k in range(NW // 4):
                w = w_nat[:, 4 * k:4 * k + 4, :]
                step.then(v.tensor_tensor(w, w, inv[:, 4 * k:4 * k + 4].unsqueeze(2).to_broadcast([P, 4, P]), ALU.mult))
                step.last()
                step.then(v.tensor_scalar(w, w, -1.0, 1.0, ALU.max, ALU.min))
                step.last()
                v.tensor_scalar(tern[:, 4 * k:4 * k + 4, :], w, ROUND, -ROUND, ALU.add, ALU.add).then_inc(ternary, 1)
            dve.wait_ge(small_in, (len(small) + len(rows)) * 16)
            step.then(v.tensor_scalar(m.qkb[:, :], m.qkb[:, :], SPLIT, None, ALU.mult))
            step.then(v.tensor_scalar(m.cw[:, :, :], m.cw[:, :, :], 0.5, None, ALU.mult))
            step.then(v.tensor_scalar(m.cb[:, :], m.cb[:, :], 0.5, None, ALU.mult))
            step.then(v.tensor_scalar(m.s1_own[:, :], m.s1[:, E * FB:], 0.5, None, ALU.mult))
            step.then(v.tensor_scalar(m.s2_own[:, :], m.s2[:, E:], 1.0 / SPLIT, None, ALU.mult))
            dve.wait_ge(projected, 3)
            step.then(v.tensor_tensor(m.bo[:, :], m.bank[4][:, 0:D], m.bo[:, :], ALU.add))

        @block.tensor
        def _(pe):
            t = nc.tensor
            pe.wait_ge(pool_made, 9)
            pe.wait_ge(dve_made, 6)
            t.matmul(m.bank[2][:, 0:2], m.ones[:, :], part_sums[:, :], start=True, stop=True).then_inc(projected, 1)
            pe.wait_ge(dve_made, 12)
            for k in range(3):
                last = t.matmul(m.bank[3][0:16, P * k:P * k + P], scale_rows[:, k, :], m.id32[:, :], start=True, stop=True,
                                is_transpose=True)
            last.then_inc(projected, 1)
            pe.wait_ge(small_in, (len(small) + len(rows)) * 16)
            t.matmul(m.bank[4][:, 0:D], m.bv[:, :].to_broadcast([P, P]), m.wo[1][:, :], start=True, stop=True).then_inc(projected, 1)
            for k in range(NW // 4):
                pe.wait_ge(ternary, k + 1)
                if k >= 2:
                    pe.wait_ge(kept, k - 1)
                for w in range(4):
                    last = t.transpose(m.bank[k % 2][:, 64 * w:64 * w + 64].bitcast(F16), tern[:, 4 * k + w, :], m.id16[:, :])
                last.then_inc(transposed, 1)


class Norm:

    def __init__(self, nc, st, sem, n):
        self.bn = st.enter_context(nc.sbuf_tensor(n + "bn", [P, GB, 6], F32))
        self.mean, self.rs, self.apart, self.pooled = (st.enter_context(nc.sbuf_tensor(n + x, [P, GB], F32))
                                                       for x in ("mean", "rs", "apart", "pooled"))
        self.stats, self.moment, self.rstd, self.normed = (sem(n + x) for x in ("stats", "moment", "rstd", "normed"))


def norm_stats(nc, dve, f, g, rows):
    dve.wait_ge(f.rstd, g.count(1))
    for b in range(GB):
        last = nc.vector.bn_stats(f.bn[:, b, :], rows(b))
    last.then_inc(f.stats, 1)


def norm_rstd(nc, m, pl, f, g):
    gp = nc.gpsimd
    even_mean, even_m2, odd_mean, odd_m2 = (f.bn[:, :, k] for k in (1, 2, 4, 5))

    def after(k):
        pl.wait_ge(f.moment, g.count(8, k))

    pl.wait_ge(f.stats, g.count(1, 1))
    pl.wait_ge(f.normed, g.count(1))
    gp.tensor_tensor(out=f.mean[:, :], in0=even_mean, in1=odd_mean, op=ALU.add).then_inc(f.moment, 1)
    gp.tensor_tensor(out=f.apart[:, :], in0=even_mean, in1=odd_mean, op=ALU.subtract).then_inc(f.moment, 1)
    gp.tensor_tensor(out=f.pooled[:, :], in0=even_m2, in1=odd_m2, op=ALU.add).then_inc(f.moment, 1)
    after(3)
    gp.tensor_tensor(out=f.apart[:, :], in0=f.apart[:, :], in1=f.apart[:, :], op=ALU.mult)
    gp.tensor_scalar(f.mean[:, :], f.mean[:, :], 0.5, None, ALU.mult).then_inc(f.moment, 1)
    after(4)
    gp.tensor_tensor(out=f.apart[:, :], in0=f.apart[:, :], in1=m.quarter[:, :], op=ALU.mult).then_inc(f.moment, 1)
    after(5)
    gp.tensor_tensor(out=f.pooled[:, :], in0=f.pooled[:, :], in1=f.apart[:, :], op=ALU.add).then_inc(f.moment, 1)
    after(6)
    gp.tensor_tensor(out=f.pooled[:, :], in0=f.pooled[:, :], in1=m.per_d[:, :], op=ALU.mult).then_inc(f.moment, 1)
    after(7)
    gp.tensor_tensor(out=f.pooled[:, :], in0=f.pooled[:, :], in1=m.eps[:, :], op=ALU.add).then_inc(f.moment, 1)
    after(8)
    gp.tensor_tensor(out=f.rs[:, :], in0=f.pooled[:, :], in1=m.minus_half[:, :], op=ALU.pow).then_inc(f.rstd, 1)


def norm_apply(nc, dve, f, g, rows, out):
    dve.wait_ge(f.rstd, g.count(1, 1))
    for b in range(GB):
        last = nc.vector.tensor_scalar(out(b), rows(b), f.mean[:, b:b + 1], f.rs[:, b:b + 1], ALU.subtract, ALU.mult)
    last.then_inc(f.normed, 1)


def group_rows(m, g):
    first = g.i * (g.span * GB) + g.off * GB
    return lambda b: m.x[:, bass.ds(first + b, 1), :].rearrange("p b d -> p (b d)")


def attention(nc, m, a, sem, layer):
    QM_LAG, NM_LAG, KM_LAG, PV_LAG, OUT_LAG = 4, 5, 6, 7, 8
    SPAN = 2 * GB
    KG = 2 if layer == 0 else H
    KR = DH if layer == 0 else D
    VN = 1 if layer == 0 else H
    exp_scale = (1.0 if layer == 0 else DH ** -0.5) / S2
    stack_dmas = 2 * TERMS if layer == 1 else 3 * TERMS
    n = f"a{layer}_"

    def s(name):
        return sem(n + name)

    ctx_in = [s("ctx_in0"), s("ctx_in1")]
    init = s("operands_cleared")
    turned_x, turned_c, xt_kept, ct_kept = s("turned_x"), s("turned_c"), s("xt_kept"), s("ct_kept")
    q_proj, k_proj, v_proj = s("q_proj"), s("k_proj"), s("v_proj")
    q_hi, k_hi, q_lo, k_lo, v_kept = s("q_hi"), s("k_hi"), s("q_lo"), s("k_lo"), s("v_kept")
    stacked, biased = s("stacked"), s("biased")
    by_query, maxed = s("scores_by_query"), s("maxed")
    max_turned, max_kept, max_in = s("max_turned"), s("max_kept"), [s("max_in0"), s("max_in1")]
    by_key, exped = s("scores_by_key"), s("exped")
    weighted, recip, o_ready = s("weighted"), s("recip"), s("o_ready")
    o_turned, ot_kept, out_proj, added = s("o_turned"), s("ot_kept"), s("out_proj"), s("added")

    with ExitStack() as st:
        def sb(name, shape, dt=F32):
            return st.enter_context(nc.sbuf_tensor(n + name, shape, dt))

        ctx_tok = [sb(f"ctx_tok{i}", [P, GB, D]) for i in range(2)]
        norm = Norm(nc, st, sem, n)
        xn = sb("xn", [P, GB, D])
        x_t = sb("x_t", [P, GT])
        c_t = sb("c_t", [P, GT])
        qk = sb("qk", [P, 2, GT])
        hi = sb("hi", [P, 2, GT], F16)
        lo = sb("lo", [P, 2, GT], F16)
        qs = [sb(f"qs{i}", [P, H, GT], F16) for i in range(2)]
        ks = [sb(f"ks{i}", [P, KG, GT], F16) for i in range(2)]
        vs = [sb(f"vs{i}", [P, GB, VN, VW]) for i in range(2)]
        nmax = [sb(f"nmax{i}", [P, H]) for i in range(2)]
        nmax_t = [sb(f"nmax_t{i}", [H, S], F16) for i in range(2)]
        prob = [sb(f"prob{i}", [P, H, S]) for i in range(2)]
        rec = [sb(f"rec{i}", [P, H]) for i in range(2)]
        o_tok = [sb(f"o_tok{i}", [P, D]) for i in range(2)]
        o_t = sb("o_t", [P, S])
        block = st.enter_context(nc.Block())

        query_bank, key_bank = m.bank[0:2], m.bank[2:4]
        turn_bank, out_bank, x_bank, c_bank = m.bank[4:8]

        @block.sync
        def _(sp):
            def step(t):
                g = t.group()
                if t.live() and t.off % GB == 0:
                    first = g.i * (2 * GB) + g.off * GB
                    first = first if isinstance(first, int) else sp.snap(first)
                    sp.wait_ge(turned_c, g.count(1, -1))
                    sp.dma_start(ctx_tok[g.slot][:, :, :], a["ctx"][bass.ds(first, GB), :, :].rearrange("b p d -> p b d")
                                 ).then_inc(ctx_in[g.slot], 16)
                if t.live() and t.off % GB == 2:
                    if g.off == 0 or g.off == 1:
                        sp.wait_ge(init, 2)
                    sp.wait_ge(q_lo, g.count(1, 1))
                    for term in range(TERMS):
                        sp.dma_start(qs[g.slot][DH * term:DH * term + DH, :, :],
                                     (hi, hi, lo, lo)[term][:, 0, :]).then_inc(stacked, 16)
                    sp.wait_ge(k_lo, g.count(1, 1))
                    for term in range(TERMS):
                        half = (hi, lo, hi, lo)[term]
                        if layer == 1:
                            sp.dma_start(ks[g.slot][DH * term:DH * term + DH, :, :], half[:, 1, :]).then_inc(stacked, 16)
                        else:
                            for k in range(KG):
                                sp.dma_start(ks[g.slot][DH * term:DH * term + DH, k, :], half[0:DH, 1, :]).then_inc(stacked, 16)
                u = t.back(NM_LAG)
                if u.live():
                    sp.wait_ge(max_kept, u.count(1, 1))
                    b0 = u.off % GB * S
                    row = qs[u.group().slot][NM:P, :, b0:b0 + S]
                    sp.dma_start(row, nmax_t[u.slot][:, :]).then_inc(max_in[u.slot], 16)

            pipeline(sp, SPAN, B, OUT_LAG, step)

        @block.gpsimd
        def _(pl):
            g_ = nc.gpsimd

            def step(t):
                g = t.group()
                if t.live() and t.off % GB == 0:
                    norm_rstd(nc, m, pl, norm, g)
                    if layer == 1:
                        pl.wait_ge(norm.normed, g.count(1, 1))
                        xg = m.x[:, bass.ds(g.i * (2 * GB) + g.off * GB, GB), :]
                        g_.tensor_tensor(out=xg, in0=xg, in1=m.bo[:, :].unsqueeze(1).to_broadcast([P, GB, D]),
                                         op=ALU.add).then_inc(biased, 1)

            pipeline(pl, SPAN, B, OUT_LAG, step)

        @block.scalar
        def _(act):
            f = nc.scalar

            def copy(out, in_, func=ACT.Copy, **more):
                return f.activation(out, in_, func, **more)

            def exp(t, u):
                if not t.live():
                    return
                act.wait_ge(by_key, t.count(4, u + 1))
                if u == 0:
                    act.wait_ge(weighted, t.count(1, -1))
                if layer == 0:
                    half, h0 = u % 2, 8 * (u // 2)
                    dst = prob[t.slot][:, h0:h0 + 8, 64 * half:64 * half + 64]
                    src = key_bank[u % 2][:, :].rearrange("p (h s) -> p h s", h=8)
                else:
                    dst = prob[t.slot][:, 4 * u:4 * u + 4, :].rearrange("p h s -> p (h s)")
                    src = key_bank[u % 2][:, :]
                copy(dst, src, ACT.Exp, scale=exp_scale).then_inc(exped, 1)

            def step(t):
                g = t.group()
                km, nm, out = t.back(KM_LAG), t.back(NM_LAG), t.back(OUT_LAG)
                exp(km, 0)
                exp(km, 1)
                if nm.live():
                    act.wait_ge(max_turned, nm.count(1, 1))
                if out.live():
                    act.wait_ge(o_turned, out.count(1, 1))
                if nm.live():
                    act.wait_ge(max_in[nm.slot], nm.arrivals(16) - 16)
                    copy(nmax_t[nm.slot][:, :], turn_bank[0:H, 0:S], scale=1.0 / S2).then_inc(max_kept, 1)
                if out.live():
                    copy(o_t[:, :], turn_bank[:, S:2 * S]).then_inc(ot_kept, 1)
                exp(km, 2)
                exp(km, 3)
                if t.live() and t.off % GB == 0:
                    act.wait_ge(turned_x, g.count(1, 1))
                    copy(x_t[:, :], x_bank[:, :]).then_inc(xt_kept, 1)
                    act.wait_ge(turned_c, g.count(1, 1))
                    copy(c_t[:, :], c_bank[:, :]).then_inc(ct_kept, 1)
                if t.live() and t.off % GB == 1:
                    act.wait_ge(stacked, g.count(16 * stack_dmas))
                    for k, rows, proj, bank, split in ((0, D, q_proj, x_bank, q_hi), (1, KR, k_proj, c_bank, k_hi)):
                        act.wait_ge((q_lo, k_lo)[k], g.count(1))
                        act.wait_ge(proj, g.count(1, 1))
                        if layer == 0:
                            copy(qk[0:rows, k, :], bank[0:rows, :], scale=SPLIT)
                            copy(hi[0:rows, k, :], bank[0:rows, :], scale=SPLIT).then_inc(split, 1)
                        else:
                            copy(qk[:, k, :], bank[:, :], ACT.Identity, scale=SPLIT, bias=m.qkb[:, k:k + 1])
                            copy(hi[:, k, :], bank[:, :], ACT.Identity, scale=SPLIT, bias=m.qkb[:, k:k + 1]).then_inc(split, 1)
                if t.live() and t.off % GB == 2:
                    act.wait_ge(v_proj, g.count(1, 1))
                    act.wait_ge(weighted, g.count(GB, -GB))
                    copy(vs[g.slot][:, :, :, 0:DH], c_bank[:, 0:GB * VN * DH].rearrange("p (b h d) -> p b h d", b=GB, h=VN)
                         ).then_inc(v_kept, 1)

            act.wait_ge(init, 1)
            pipeline(act, SPAN, B, OUT_LAG, step)

        @block.vector
        def _(dve):
            v = nc.vector

            def row_max(t, u):
                if not t.live():
                    return
                dve.wait_ge(by_query, t.count(4, u + 1))
                if u == 0:
                    dve.wait_ge(max_turned, t.count(1, -1))
                dst = nmax[t.slot][:, 4 * u:4 * u + 4]
                src = query_bank[u % 2][:, :].rearrange("p (h k) -> p h k", h=4)
                v.tensor_reduce(dst, src, AX.X, ALU.max, negate=True).then_inc(maxed, 1)

            def step(t):
                g = t.group()
                qm, pv, out = t.back(QM_LAG), t.back(PV_LAG), t.back(OUT_LAG)
                front = t.live() and t.off % GB == 0
                rows = group_rows(m, g)
                if front:
                    if layer == 0 and isinstance(g.i, int) and g.off == 0:
                        dve.wait_ge(m.x_in, 16 * NG)
                    norm_stats(nc, dve, norm, g, rows)
                row_max(qm, 0)
                row_max(qm, 1)
                if front:
                    dve.wait_ge(turned_x, g.count(1))
                    norm_apply(nc, dve, norm, g, rows, lambda b: xn[:, b, :])
                if t.live() and t.off % GB == 2:
                    for k, used, split, done in ((0, D, q_hi, q_lo), (1, KR, k_hi, k_lo)):
                        dve.wait_ge(split, g.count(1, 1))
                        v.tensor_tensor(lo[0:used, k, :], qk[0:used, k, :], hi[0:used, k, :], ALU.subtract).then_inc(done, 1)
                row_max(qm, 2)
                row_max(qm, 3)
                if pv.live():
                    dve.wait_ge(weighted, pv.count(1, 1))
                if out.live():
                    dve.wait_ge(out_proj, out.count(1, 1))
                if pv.live():
                    wv = out_bank[:, 0:H * VW].rearrange("p (h w) -> p h w", h=H)
                    v.reciprocal(rec[pv.slot][:, :], wv[:, :, DH]).then_inc(recip, 1)
                    dve.wait_ge(o_turned, pv.count(1, -1))
                    dve.wait_ge(recip, pv.count(1, 1))
                    v.tensor_tensor(o_tok[pv.slot][:, :].rearrange("p (h d) -> p h d", h=H), wv[:, :, 0:DH],
                                    rec[pv.slot][:, :].unsqueeze(2).to_broadcast([P, H, DH]), ALU.mult).then_inc(o_ready, 1)
                if out.live():
                    if layer == 1:
                        dve.wait_ge(biased, out.group().count(1, 1))
                    xb = m.x[:, bass.ds(out.count(1), 1), :].rearrange("p b d -> p (b d)")
                    v.tensor_tensor(xb, out_bank[:, 256:256 + D], xb, ALU.add).then_inc(added, 1)

            for i in range(2):
                last = v.memset(vs[i][:, :, :, :].rearrange("p b h w -> p (b h w)"), 1.0)
            last.then_inc(init, 1)
            for i in range(2):
                v.tensor_copy(qs[i][:, :, :].rearrange("p h (b s) -> p (h b) s", b=GB),
                              m.band_q[:, :, :].rearrange("p f s -> p (f s)").unsqueeze(1).to_broadcast([P, H * GB, S]))
                if layer == 0:
                    last = v.tensor_copy(ks[i][:, :, :].rearrange("p f (b s) -> p f b s", b=GB),
                                         m.band_k[:, :, :].unsqueeze(2).to_broadcast([P, 2, GB, S]))
                else:
                    last = v.tensor_copy(ks[i][:, :, :].rearrange("p h (b s) -> p (h b) s", b=GB),
                                         m.plain_k[:, :].unsqueeze(1).to_broadcast([P, H * GB, S]))
            last.then_inc(init, 1)
            pipeline(dve, SPAN, B, OUT_LAG, step)

        @block.tensor
        def _(pe):
            mm = nc.tensor

            def scores_by_query(t, u):
                if not t.live():
                    return
                q, k, b0 = qs[t.group().slot], ks[t.group().slot], t.off % GB * S
                if u == 0:
                    pe.wait_ge(stacked, t.group().count(16 * stack_dmas, 16 * stack_dmas))
                pe.wait_ge(maxed, t.count(4, u - 1))
                for j in range(4):
                    h, dst = 4 * u + j, query_bank[u % 2][:, S * j:S * j + S]
                    if layer == 0:
                        for half in range(2):
                            last = mm.matmul(dst[64 * half:64 * half + 64, :], q[0:NM, h, b0 + 64 * half:b0 + 64 * half + 64],
                                             k[0:NM, half, b0:b0 + S], start=True, stop=True)
                    else:
                        last = mm.matmul(dst, q[0:NM, h, b0:b0 + S], k[0:NM, h, b0:b0 + S], start=True, stop=True)
                last.then_inc(by_query, 1)

            def scores_by_key(t, u):
                if not t.live():
                    return
                q, k, b0 = qs[t.group().slot], ks[t.group().slot], t.off % GB * S
                if u == 0:
                    pe.wait_ge(max_in[t.slot], t.arrivals(16))
                pe.wait_ge(exped, t.count(4, u - 1))
                if layer == 0:
                    half, h0 = u % 2, 8 * (u // 2)
                    last = mm.matmul(key_bank[u % 2][:, :], k[:, half, b0:b0 + S],
                                     q[:, h0:h0 + 8, b0 + 64 * half:b0 + 64 * half + 64], start=True, stop=True)
                else:
                    for j in range(4):
                        last = mm.matmul(key_bank[u % 2][:, S * j:S * j + S], k[:, 4 * u + j, b0:b0 + S],
                                         q[:, 4 * u + j, b0:b0 + S], start=True, stop=True)
                last.then_inc(by_key, 1)

            def step(t):
                g = t.group()
                qm, nm, km, pv, out = (t.back(lag) for lag in (QM_LAG, NM_LAG, KM_LAG, PV_LAG, OUT_LAG))
                for u in range(2):
                    scores_by_query(qm, u)
                    scores_by_key(km, u)
                if nm.live() or out.live():
                    if nm.back(1).live():
                        pe.wait_ge(max_kept, nm.count(1))
                    if out.back(1).live():
                        pe.wait_ge(ot_kept, out.count(1))
                if nm.live():
                    pe.wait_ge(maxed, nm.count(4, 4))
                    mm.transpose(turn_bank[0:H, 0:S], nmax[nm.slot][:, :], m.id32[:, :]).then_inc(max_turned, 1)
                if out.live():
                    pe.wait_ge(o_ready, out.count(1, 1))
                    mm.transpose(turn_bank[:, S:2 * S], o_tok[out.slot][:, :], m.id32[:, :]).then_inc(o_turned, 1)
                for u in range(2, 4):
                    scores_by_query(qm, u)
                    scores_by_key(km, u)
                if t.live() and t.off % GB == 0:
                    pe.wait_ge(norm.normed, g.count(1, 1))
                    pe.wait_ge(q_hi, g.count(1))
                    for b in range(GB):
                        last = mm.transpose(x_bank[:, S * b:S * b + S], xn[:, b, :], m.id32[:, :])
                    last.then_inc(turned_x, 1)
                    pe.wait_ge(ctx_in[g.slot], g.arrivals(16))
                    pe.wait_ge(v_kept, g.count(1))
                    for b in range(GB):
                        last = mm.transpose(c_bank[:, S * b:S * b + S], ctx_tok[g.slot][:, b, :], m.id32[:, :])
                    last.then_inc(turned_c, 1)
                if t.live() and t.off % GB == 1:
                    pe.wait_ge(xt_kept, g.count(1, 1))
                    mm.matmul(x_bank[:, :], m.wq[layer][:, :], x_t[:, :], start=True, stop=True).then_inc(q_proj, 1)
                    pe.wait_ge(ct_kept, g.count(1, 1))
                    mm.matmul(c_bank[0:KR, :], m.wk[layer][:, :], c_t[:, :], start=True, stop=True).then_inc(k_proj, 1)
                if t.live() and t.off % GB == 2:
                    pe.wait_ge(k_hi, g.count(1, 1))
                    w = VN * DH
                    for b in range(GB):
                        last = mm.matmul(c_bank[:, w * b:w * b + w], c_t[:, S * b:S * b + S], m.wv[layer][:, :],
                                         start=True, stop=True)
                    last.then_inc(v_proj, 1)
                if pv.live() or out.live():
                    if pv.back(1).live():
                        pe.wait_ge(o_ready, pv.count(1))
                    if out.back(1).live():
                        pe.wait_ge(added, out.count(1))
                if pv.live():
                    pg = pv.group()
                    pe.wait_ge(exped, pv.count(4, 4))
                    if pv.off % GB == 0:
                        pe.wait_ge(v_kept, pg.count(1, 1))
                    for h in range(H):
                        last = mm.matmul(out_bank[:, VW * h:VW * h + VW], prob[pv.slot][:, h, :],
                                         vs[pg.slot][:, pv.off % GB, h % VN, :], start=True, stop=True)
                    last.then_inc(weighted, 1)
                if out.live():
                    pe.wait_ge(ot_kept, out.count(1, 1))
                    mm.matmul(out_bank[:, 256:256 + D], o_t[:, :], m.wo[layer][:, :], start=True, stop=True).then_inc(out_proj, 1)

            pe.wait_ge(init, 2)
            pipeline(pe, SPAN, B, OUT_LAG, step)


def expert_ffn(nc, m, a, sem):
    UP_LAG, DOWN_LAG, SPAN = 1, 2, 2
    ROUTE = 12
    n = "e_"

    def s(name):
        return sem(n + name)

    h_step, h_ready = s("h_step"), s("h_ready")
    head_tile, head_kept, lo_ready = s("head_tile"), s("head_kept"), s("lo_ready")
    route_tile, route_kept = s("route_tile"), s("route_kept")
    router, exped, onehot = s("router"), s("exped"), s("onehot")
    masked, up_used = s("masked"), s("up_used")
    z_scaled, z_own, tanhed, gated, h1_hi, h1_lo = s("z_scaled"), s("z_own"), s("tanhed"), s("gated"), s("h1_hi"), s("h1_lo")
    h1_masked, down_used = s("h1_masked"), s("down_used")
    y_step, y_ready, y_turned, added = s("y_step"), s("y_ready"), s("y_turned"), s("added")

    with ExitStack() as st:
        def sb(name, shape, dt=F32):
            return st.enter_context(nc.sbuf_tensor(n + name, shape, dt))

        first_norm = Norm(nc, st, sem, n + "n1_")
        second_norm = Norm(nc, st, sem, n + "n2_")
        xn = sb("xn", [P, GB, D])
        hn = sb("hn", [P, GB, D])
        h_t = sb("h_t", [P, GT])
        h_half = [sb(f"h_half{i}", [P, 2, GT], F16) for i in range(2)]
        logits = sb("logits", [P, GB, E])
        below = sb("below", [P, GB, E])
        ex = sb("ex", [P, GB, E])
        cand = sb("cand", [P, GB, E])
        top = sb("top", [P, 3, GB])
        choice = sb("choice", [P, GB, 2 * E])
        masks = [sb(f"masks{i}", [P, E, GT], F16) for i in range(2)]
        s1_tok = sb("s1_tok", [P, FB, GT])
        s2_tok = [sb(f"s2_tok{i}", [P, GT]) for i in range(2)]
        hm = [sb(f"hm{i}", [P, 2, GT], F16) for i in range(2)]
        z = sb("z", [P, 2 * FB, GT])
        th = sb("th", [P, 2 * FB, GT])
        h1 = sb("h1", [P, 2, 2 * FB, GT], F16)
        h1m = [sb(f"h1m{i}", [P, 2, GT], F16) for i in range(4)]
        routed = sb("routed", [P, GT])
        y = sb("y", [P, GT])
        block = st.enter_context(nc.Block())

        up_bank, down_bank, front_bank = m.bank[0:4], m.bank[4:6], m.bank[6:8]

        @block.gpsimd
        def _(pl):
            def step(t):
                if not t.live():
                    return
                norm_rstd(nc, m, pl, first_norm, t)
                norm_rstd(nc, m, pl, second_norm, t)
                pl.wait_ge(second_norm.normed, t.count(1, 1))
                nc.gpsimd.tensor_tensor(out=hn[:, :, :], in0=hn[:, :, :],
                                        in1=m.gamma[:, :].unsqueeze(1).to_broadcast([P, GB, D]), op=ALU.mult).then_inc(h_step, 1)
                pl.wait_ge(h_step, t.count(1, 1))
                nc.gpsimd.tensor_tensor(out=hn[:, :, :], in0=hn[:, :, :],
                                        in1=m.beta[:, :].unsqueeze(1).to_broadcast([P, GB, D]), op=ALU.add).then_inc(h_ready, 1)

            pipeline(pl, SPAN, NG, DOWN_LAG, step)

        @block.vector
        def _(dve):
            v = nc.vector

            def mask_up(g, e):
                if g.live():
                    dve.wait_ge(route_kept, g.count(ROUTE, 2 + e))
                    dve.wait_ge(lo_ready, g.count(1, 1))
                    dve.wait_ge(up_used, g.count(E, e - 1))
                    v.tensor_tensor(hm[e % 2][:, :, :], h_half[g.slot][:, :, :],
                                    masks[g.slot][:, e, :].unsqueeze(1).to_broadcast([P, 2, GT]), ALU.mult).then_inc(masked, 1)

            def mask_down(g, e):
                if g.live():
                    dve.wait_ge(h1_lo, g.count(2 * FB, 2 * FB))
                    for f in range(FB):
                        k = FB * e + f
                        dve.wait_ge(down_used, g.count(FB * E, max(k - 3, 0)))
                        v.tensor_tensor(h1m[k % 4][:, :, :], h1[:, :, f, :],
                                        masks[g.slot][:, e, :].unsqueeze(1).to_broadcast([P, 2, GT]), ALU.mult).then_inc(h1_masked, 1)

            def route(g, part):
                if not g.live():
                    return

                def done(k, ins):
                    ins.then_inc(router, 1)

                def after(k):
                    dve.wait_ge(router, g.count(7, k))

                if part == 0:
                    dve.wait_ge(head_kept, g.count(2, 2))
                    done(1, v.tensor_reduce(top[:, 0, :], logits[:, :, :], AX.X, ALU.max))
                    after(1)
                    done(2, v.tensor_tensor(below[:, :, :], logits[:, :, :], top[:, 0, :].unsqueeze(2).to_broadcast([P, GB, E]),
                                            ALU.subtract))
                    after(2)
                    done(3, v.scalar_tensor_tensor(cand[:, :, :], below[:, :, :], 0.0,
                                                   m.rank[:, :].unsqueeze(1).to_broadcast([P, GB, E]), ALU.is_ge, ALU.mult))
                    after(3)
                    done(4, v.tensor_reduce(top[:, 1, :], cand[:, :, :], AX.X, ALU.max))
                else:
                    after(4)
                    dve.wait_ge(route_tile, g.count(ROUTE, 1 - ROUTE))
                    done(5, v.tensor_tensor(choice[:, :, 0:E], cand[:, :, :], top[:, 1, :].unsqueeze(2).to_broadcast([P, GB, E]),
                                            ALU.is_equal))
                    dve.wait_ge(exped, g.count(1, 1))
                    done(6, v.tensor_reduce(top[:, 2, :], ex[:, :, :], AX.X, ALU.add))
                    after(6)
                    done(7, v.reciprocal(top[:, 2, :], top[:, 2, :]))
                    after(7)
                    v.tensor_tensor(choice[:, :, E:], choice[:, :, 0:E], top[:, 2, :].unsqueeze(2).to_broadcast([P, GB, E]),
                                    ALU.mult).then_inc(onehot, 1)

            def step(t):
                up, down = t.back(UP_LAG), t.back(DOWN_LAG)
                head = t.live()
                rows = group_rows(m, t)
                if head:
                    norm_stats(nc, dve, first_norm, t, rows)
                for e in range(E):
                    mask_up(up, e)
                    mask_down(down, e)
                    if head and e == 0:
                        norm_apply(nc, dve, first_norm, t, rows, lambda b: xn[:, b, :])
                    if head and e == 1:
                        dve.wait_ge(first_norm.normed, t.count(1, 1))
                        norm_stats(nc, dve, second_norm, t, lambda b: xn[:, b, :])
                    if head and e == 2:
                        dve.wait_ge(head_tile, t.count(2, -1))
                        norm_apply(nc, dve, second_norm, t, lambda b: xn[:, b, :], lambda b: hn[:, b, :])
                    if head and e == 6:
                        dve.wait_ge(head_kept, t.count(2, 1))
                        v.tensor_tensor(h_half[t.slot][:, 1, :], h_t[:, :], h_half[t.slot][:, 0, :], ALU.subtract).then_inc(lo_ready, 1)
                    if e == 7:
                        route(t, 0)
                if down.live():
                    dve.wait_ge(down_used, down.count(FB * E, FB * E))
                    dve.wait_ge(route_kept, down.count(ROUTE, 12))
                    v.tensor_tensor(routed[:, :], down_bank[0][:, :], s2_tok[down.slot][:, :], ALU.mult).then_inc(y_step, 1)
                    dve.wait_ge(y_step, down.count(1, 1))
                    dve.wait_ge(y_turned, down.count(1))
                    v.scalar_tensor_tensor(y[:, :], down_bank[1][:, :], m.s2_own[:, 0:1], routed[:, :], ALU.mult, ALU.add
                                           ).then_inc(y_ready, 1)
                if up.live():
                    dve.wait_ge(up_used, up.count(E, E))
                    dve.wait_ge(route_kept, up.count(ROUTE, 11))
                    dve.wait_ge(tanhed, up.count(2 * FB))
                    for f in range(FB):
                        v.tensor_tensor(z[:, f, :], up_bank[f][:, :], s1_tok[:, f, :], ALU.mult).then_inc(z_scaled, 1)
                route(t, 1)
                if up.live():
                    for f in range(2 * FB):
                        dve.wait_ge(tanhed, up.count(2 * FB, f + 1))
                        v.scalar_tensor_tensor(th[:, f, :], th[:, f, :], 1.0, z[:, f, :], ALU.add, ALU.mult).then_inc(gated, 1)
                    for f in range(2 * FB):
                        dve.wait_ge(h1_hi, up.count(2 * FB, f + 1))
                        v.tensor_tensor(h1[:, 1, f, :], th[:, f, :], h1[:, 0, f, :], ALU.subtract).then_inc(h1_lo, 1)
                if down.live():
                    dve.wait_ge(y_turned, down.count(1, 1))
                    xg = m.x[:, bass.ds(down.count(GB), GB), :].rearrange("p b d -> p (b d)")
                    v.tensor_tensor(xg, down_bank[0][:, :], xg, ALU.add).then_inc(added, 1)

            pipeline(dve, SPAN, NG, DOWN_LAG, step)

        @block.scalar
        def _(act):
            f_ = nc.scalar

            def kept(g, k):
                act.wait_ge(route_tile, g.count(ROUTE, k + 1))

            def step(t):
                up = t.back(UP_LAG)
                if up.live():
                    kept(up, 0)
                    f_.activation(m.o_t32[0:2 * E, :], front_bank[0][0:2 * E, :], ACT.Copy)
                    f_.activation(m.o_t16[0:2 * E, :], front_bank[0][0:2 * E, :], ACT.Copy).then_inc(route_kept, 1)
                    act.wait_ge(h1_masked, up.count(FB * E, -FB * E))
                    for e in range(E):
                        kept(up, 1 + e)
                        f_.activation(masks[up.slot][:, e, :], front_bank[(1 + e) % 2][:, :], ACT.Copy).then_inc(route_kept, 1)
                    act.wait_ge(z_scaled, up.count(FB))
                    for f in range(FB):
                        kept(up, 9 + f)
                        f_.activation(s1_tok[:, f, :], front_bank[(9 + f) % 2][:, :], ACT.Copy).then_inc(route_kept, 1)
                    kept(up, 11)
                    act.wait_ge(y_step, up.count(1, -1))
                    f_.activation(s2_tok[up.slot][:, :], front_bank[1][:, :], ACT.Copy).then_inc(route_kept, 1)
                if t.live():
                    act.wait_ge(head_tile, t.count(2, 1))
                    act.wait_ge(lo_ready, t.count(1))
                    act.wait_ge(up_used, t.count(E, -E))
                    f_.activation(h_t[:, :], front_bank[0][:, :], ACT.Copy, scale=SPLIT)
                    f_.activation(h_half[t.slot][:, 0, :], front_bank[0][:, :], ACT.Copy, scale=SPLIT).then_inc(head_kept, 1)
                    act.wait_ge(head_tile, t.count(2, 2))
                    f_.activation(logits[:, :, :].rearrange("p b e -> p (b e)"), front_bank[1][:, 0:GB * E], ACT.Copy
                                  ).then_inc(head_kept, 1)
                    act.wait_ge(router, t.count(7, 2))
                    f_.activation(ex[:, :, :].rearrange("p b e -> p (b e)"), below[:, :, :].rearrange("p b e -> p (b e)"),
                                  ACT.Exp, scale=1.0 / SPLIT).then_inc(exped, 1)
                if up.live():
                    act.wait_ge(up_used, up.count(E, E))
                    act.wait_ge(gated, up.count(2 * FB))
                    for f in range(FB):
                        f_.activation(z[:, FB + f, :], up_bank[FB + f][:, :], ACT.Identity, scale=m.s1_own[:, f:f + 1]
                                      ).then_inc(z_own, 1)
                    act.wait_ge(z_own, up.count(FB, FB))
                    act.wait_ge(z_scaled, up.count(FB, FB))
                    act.wait_ge(h1_lo, up.count(2 * FB))
                    for f in range(2 * FB):
                        f_.activation(th[:, f, :], z[:, f, :], ACT.Tanh, scale=1.0 / SPLIT).then_inc(tanhed, 1)
                    act.wait_ge(down_used, up.count(FB * E))
                    act.wait_ge(h1_masked, up.count(FB * E))
                    for f in range(2 * FB):
                        act.wait_ge(gated, up.count(2 * FB, f + 1))
                        f_.activation(h1[:, 0, f, :], th[:, f, :], ACT.Copy).then_inc(h1_hi, 1)

            pipeline(act, SPAN, NG, DOWN_LAG, step)

        @block.tensor
        def _(pe):
            mm = nc.tensor

            def tile(g, k):
                if k >= 2:
                    pe.wait_ge(route_kept, g.count(ROUTE, k - 1))
                return front_bank[k % 2]

            def mask(g, e):
                if g.live():
                    mm.matmul(tile(g, 1 + e)[:, :], m.pick[:, e, :], m.o_t16[:, :], start=True, stop=True).then_inc(route_tile, 1)

            def step(t):
                up, down = t.back(UP_LAG), t.back(DOWN_LAG)
                if up.live():
                    pe.wait_ge(onehot, up.count(1, 1))
                    pe.wait_ge(head_kept, up.count(2, 2))
                    for b in range(GB):
                        last = mm.transpose(tile(up, 0)[0:2 * E, S * b:S * b + S], choice[:, b, :], m.id32[:, :])
                    last.then_inc(route_tile, 1)
                    pe.wait_ge(lo_ready, up.count(1, 1))
                    pe.wait_ge(z_scaled, up.count(FB))
                    pe.wait_ge(z_own, up.count(FB))
                    for f in range(FB):
                        for part in range(2):
                            mm.matmul(up_bank[FB + f][:, :], m.w_t[:, W1S + f, :], h_half[up.slot][:, part, :],
                                      start=part == 0, stop=part == 1)
                    pe.wait_ge(route_kept, up.count(ROUTE, 1))
                mask(up, 0)
                mask(up, 1)
                if down.live():
                    pe.wait_ge(h1_lo, down.count(2 * FB, 2 * FB))
                    pe.wait_ge(y_ready, down.count(1))
                    for f in range(FB):
                        for part in range(2):
                            mm.matmul(down_bank[1][:, :], m.w_t[:, W2S + f, :], h1[:, part, FB + f, :],
                                      start=f + part == 0, stop=f + part == 2)
                    pe.wait_ge(added, down.count(1))
                for e in range(E):
                    if up.live():
                        pe.wait_ge(masked, up.count(E, e + 1))
                        for f in range(FB):
                            for part in range(2):
                                last = mm.matmul(up_bank[f][:, :], m.w_t[:, W1E + FB * e + f, :], hm[e % 2][:, part, :],
                                                 start=e + part == 0, stop=e + part == E)
                        last.then_inc(up_used, 1)
                    if e < 3:
                        mask(up, 2 + 2 * e)
                        mask(up, 3 + 2 * e)
                    if e == 3 and up.live():
                        for f in range(FB):
                            mm.matmul(tile(up, 9 + f)[:, :], m.s1_t[:, f, :], m.o_t32[:, :], start=True, stop=True).then_inc(route_tile, 1)
                    if e == 4 and up.live():
                        mm.matmul(tile(up, 11)[:, :], m.s2_t[:, :], m.o_t32[:, :], start=True, stop=True).then_inc(route_tile, 1)
                    if e == 5 and t.live():
                        pe.wait_ge(h_ready, t.count(1, 1))
                        pe.wait_ge(route_kept, t.count(ROUTE))
                        for b in range(GB):
                            last = mm.transpose(front_bank[0][:, S * b:S * b + S], hn[:, b, :], m.id32[:, :])
                        last.then_inc(head_tile, 1)
                    if e == 6 and t.live():
                        pe.wait_ge(head_kept, t.count(2, 1))
                        for b in range(GB):
                            last = mm.matmul(front_bank[1][:, E * b:E * b + E], h_t[:, S * b:S * b + S], m.rw[:, :], start=True, stop=True)
                        last.then_inc(head_tile, 1)
                    if down.live():
                        for f in range(FB):
                            pe.wait_ge(h1_masked, down.count(FB * E, FB * e + f + 1))
                            for part in range(2):
                                k = 2 * (FB * e + f) + part
                                last = mm.matmul(down_bank[0][:, :], m.w_t[:, W2E + FB * e + f, :], h1m[(FB * e + f) % 4][:, part, :],
                                                 start=k == 0, stop=k == 2 * FB * E - 1)
                            last.then_inc(down_used, 1)
                if down.live():
                    pe.wait_ge(y_step, down.count(1, 1))
                    pe.wait_ge(y_ready, down.count(1, 1))
                    for b in range(GB):
                        last = mm.transpose(down_bank[0][:, S * b:S * b + S], y[:, S * b:S * b + S], m.id32[:, :])
                    last.then_inc(y_turned, 1)

            pipeline(pe, SPAN, NG, DOWN_LAG, step)


def conv_ffn(nc, m, a, sem, out):
    UP_LAG, DOWN_LAG, SPAN = 1, 2, 2
    n = "c_"

    def s(name):
        return sem(n + name)

    quant, levels, by_token, head_used = s("quant"), s("levels"), s("by_token"), s("head_used")
    q_turned, q_kept, r_spread, r_kept = s("q_turned"), s("q_kept"), s("r_spread"), s("r_kept")
    uped, scaled, centred, left, right, tanhed, hidden = (s(x) for x in ("uped", "scaled", "centred", "left", "right", "tanhed", "hidden"))
    h_turned, requant, clipped, h_levels = s("h_turned"), s("requant"), s("clipped"), s("h_levels")
    l_turned, l_kept, downed, added, stored = s("l_turned"), s("l_kept"), s("downed"), s("added"), s("stored")

    with ExitStack() as st:
        def sb(name, shape, dt=F32):
            return st.enter_context(nc.sbuf_tensor(n + name, shape, dt))

        norm = Norm(nc, st, sem, n)
        xn = sb("xn", [P, GB, D])
        amax = sb("amax", [P, 3, GB])
        back = [sb(f"back{i}", [P, GB]) for i in range(2)]
        whole = sb("whole", [P, GB, D])
        lev = sb("lev", [P, GB, D], F16)
        lev_t = sb("lev_t", [P, GT], F16)
        r_tok = sb("r_tok", [P, GT])
        zp = sb("zp", [P, CB, GB, S + 2])
        yc = sb("yc", [P, CB, GT])
        th = sb("th", [P, CB, GT])
        hid = [sb(f"hid{i}", [P, CB, GT]) for i in range(2)]
        amax2 = [sb(f"amax2_{i}", [P, 4]) for i in range(2)]
        whole2 = [sb(f"whole2_{i}", [P, CF]) for i in range(2)]
        lev2 = [sb(f"lev2_{i}", [P, CF], F16) for i in range(2)]
        lev2_t = [sb(f"lev2_t{i}", [P, CB, S], F16) for i in range(2)]
        block = st.enter_context(nc.Block())

        up_bank, head_bank, level_bank, hid_bank, down_bank = m.bank[0:4], m.bank[4], m.bank[5], m.bank[6], m.bank[7]

        @block.sync
        def _(sp):
            def step(t):
                g = t.back(DOWN_LAG)
                if g.live():
                    sp.wait_ge(added, g.count(GB, GB))
                    sp.dma_start(out[bass.ds(g.count(GB), GB), :, :].rearrange("b p d -> p b d"),
                                 m.x[:, bass.ds(g.count(GB), GB), :]).then_inc(stored, 16)

            pipeline(sp, SPAN, NG, DOWN_LAG, step)
            sp.wait_ge(stored, 16 * NG)

        @block.gpsimd
        def _(pl):
            def step(t):
                if t.live():
                    norm_rstd(nc, m, pl, norm, t)

            pipeline(pl, SPAN, NG, DOWN_LAG, step)

        @block.vector
        def _(dve):
            v = nc.vector

            def eight_bits(g):
                dve.wait_ge(norm.normed, g.count(1, 1))

                def done(ins):
                    ins.then_inc(quant, 1)

                def after(k):
                    dve.wait_ge(quant, g.count(5, k))

                done(v.tensor_reduce(amax[:, 0, :], xn[:, :, :], AX.X, ALU.max, apply_absolute_value=True))
                after(1)
                done(v.tensor_scalar(amax[:, 1, :], amax[:, 0, :], EPS, None, ALU.max))
                after(2)
                done(v.reciprocal(amax[:, 2, :], amax[:, 1, :]))
                dve.wait_ge(r_spread, g.count(1, -1))
                done(v.tensor_scalar(back[g.slot][:, :], amax[:, 1, :], m.sc[:, 0:1], 1.0 / 127.0, ALU.mult, ALU.mult))
                after(3)
                done(v.tensor_scalar(amax[:, 2, :], amax[:, 2, :], 127.0, None, ALU.mult))
                after(5)
                for b in range(GB):
                    last = v.tensor_scalar(xn[:, b, :], xn[:, b, :], amax[:, 2, b:b + 1], 127.0, ALU.mult, ALU.min)
                last.then_inc(levels, 1)
                dve.wait_ge(levels, g.count(2, 1))
                dve.wait_ge(by_token, g.count(1))
                v.tensor_scalar(whole[:, :, :], xn[:, :, :], -128.0, ROUND, ALU.max, ALU.add).then_inc(levels, 1)

            def down_levels(g, b):
                if not g.live():
                    return
                sl = b % 2
                am = amax2[sl]
                dve.wait_ge(h_turned, g.count(GB, b + 1))
                bank = hid_bank[:, :]

                def after(k):
                    dve.wait_ge(requant, g.count(5 * GB, 5 * b + k))

                v.tensor_reduce(am[:, 0:1], bank, AX.X, ALU.max, apply_absolute_value=True).then_inc(requant, 1)
                after(1)
                v.tensor_scalar(am[:, 1:2], am[:, 0:1], EPS, None, ALU.max).then_inc(requant, 1)
                after(2)
                v.reciprocal(am[:, 2:3], am[:, 1:2]).then_inc(requant, 1)
                v.tensor_scalar(am[:, 3:4], am[:, 1:2], m.sc[:, 1:2], 1.0 / 127.0, ALU.mult, ALU.mult).then_inc(requant, 1)
                after(3)
                v.tensor_scalar(am[:, 2:3], am[:, 2:3], 127.0, None, ALU.mult).then_inc(requant, 1)
                after(5)
                dve.wait_ge(h_levels, g.count(GB, max(b - 1, 0)))
                v.tensor_scalar(whole2[sl][:, :], bank, am[:, 2:3], 127.0, ALU.mult, ALU.min).then_inc(clipped, 1)
                dve.wait_ge(clipped, g.count(2 * GB, 2 * b + 1))
                v.tensor_scalar(whole2[sl][:, :], whole2[sl][:, :], -128.0, ROUND, ALU.max, ALU.add).then_inc(clipped, 1)

            def down_add(g, b):
                if not g.live():
                    return
                dve.wait_ge(downed, g.count(GB, b + 1))
                xb = m.x[:, bass.ds(g.count(GB, b), 1), :].rearrange("p b d -> p (b d)")
                v.scalar_tensor_tensor(xb, down_bank[:, 0:D], amax2[b % 2][:, 3:4], xb, ALU.mult, ALU.add).then_inc(added, 1)

            def step(t):
                up, down = t.back(UP_LAG), t.back(DOWN_LAG)
                rows = group_rows(m, t)
                if t.live():
                    norm_stats(nc, dve, norm, t, rows)
                for k in range(CB):
                    down_levels(down, k)
                    if up.live():
                        dve.wait_ge(uped, up.count(CB, k + 1))
                        dve.wait_ge(r_kept, up.count(1, 1))
                        dve.wait_ge(centred, up.count(CB, k - CB + 1))
                        v.tensor_tensor(zp[:, k, :, 1:S + 1], up_bank[k][:, :].rearrange("p (b s) -> p b s", b=GB),
                                        r_tok[:, :].rearrange("p (b s) -> p b s", b=GB), ALU.mult).then_inc(scaled, 1)
                    if k == 0 and t.live():
                        dve.wait_ge(levels, t.count(2))
                        norm_apply(nc, dve, norm, t, rows, lambda b: xn[:, b, :])
                    if k >= 1:
                        down_add(down, k - 1)
                    if up.live() and k >= 1:
                        taps(up, k - 1)
                down_add(down, CB - 1)
                if t.live():
                    eight_bits(t)
                if up.live():
                    taps(up, CB - 1)
                    for k in range(CB):
                        dve.wait_ge(tanhed, up.count(CB, k + 1))
                        dve.wait_ge(h_turned, up.count(GB, -GB))
                        v.scalar_tensor_tensor(hid[up.slot][:, k, :], th[:, k, :], 1.0, yc[:, k, :], ALU.add, ALU.mult
                                               ).then_inc(hidden, 1)

            def taps(g, k):
                y3 = yc[:, k, :].rearrange("p (b s) -> p b s", b=GB)
                dve.wait_ge(centred, g.count(CB, k + 1))
                v.scalar_tensor_tensor(y3, zp[:, k, :, 0:S], m.cw[:, k, 0:1], y3, ALU.mult, ALU.add).then_inc(left, 1)
                dve.wait_ge(left, g.count(CB, k + 1))
                v.scalar_tensor_tensor(y3, zp[:, k, :, 2:S + 2], m.cw[:, k, 2:3], y3, ALU.mult, ALU.add).then_inc(right, 1)

            v.memset(zp[:, :, :, :].rearrange("p c b s -> p (c b s)"), 0.0).then_inc(head_used, 1)
            dve.wait_ge(head_used, 1)
            pipeline(dve, SPAN, NG, DOWN_LAG, step)

        @block.scalar
        def _(act):
            f_ = nc.scalar

            def step(t):
                up, down = t.back(UP_LAG), t.back(DOWN_LAG)
                for k in range(CB):
                    if up.live():
                        act.wait_ge(scaled, up.count(CB, k + 1))
                        act.wait_ge(hidden, up.count(CB, k + 1 - CB))
                        f_.activation(yc[:, k, :].rearrange("p (b s) -> p b s", b=GB), zp[:, k, :, 1:S + 1], ACT.Identity,
                                      scale=m.cw[:, k, 1:2], bias=m.cb[:, k:k + 1]).then_inc(centred, 1)
                    if down.live():
                        act.wait_ge(clipped, down.count(2 * GB, 2 * k + 2))
                        act.wait_ge(l_turned, down.count(GB, max(k - 1, 0)))
                        f_.activation(lev2[k % 2][:, :], whole2[k % 2][:, :], ACT.Copy, bias=-ROUND).then_inc(h_levels, 1)
                        act.wait_ge(l_turned, down.count(GB, k + 1))
                        act.wait_ge(downed, down.count(GB, max(k - 1, 0)))
                        f_.activation(lev2_t[k % 2][:, :, :].rearrange("p c s -> p (c s)"), level_bank[:, 0:256].bitcast(F16),
                                      ACT.Copy).then_inc(l_kept, 1)
                if t.live():
                    act.wait_ge(levels, t.count(2, 2))
                    act.wait_ge(q_turned, t.count(1))
                    f_.activation(lev[:, :, :].rearrange("p b d -> p (b d)"), whole[:, :, :].rearrange("p b d -> p (b d)"),
                                  ACT.Copy, bias=-ROUND).then_inc(by_token, 1)
                    act.wait_ge(q_turned, t.count(1, 1))
                    act.wait_ge(uped, t.count(CB))
                    f_.activation(lev_t[:, :], head_bank[:, 0:256].bitcast(F16), ACT.Copy).then_inc(q_kept, 1)
                    act.wait_ge(r_spread, t.count(1, 1))
                    act.wait_ge(scaled, t.count(CB))
                    f_.activation(r_tok[:, :], head_bank[:, :], ACT.Copy).then_inc(r_kept, 1)
                if up.live():
                    for k in range(CB):
                        act.wait_ge(right, up.count(CB, k + 1))
                        act.wait_ge(hidden, up.count(CB, k + 1 - CB))
                        f_.activation(th[:, k, :], yc[:, k, :], ACT.Tanh).then_inc(tanhed, 1)

            pipeline(act, SPAN, NG, DOWN_LAG, step)

        @block.tensor
        def _(pe):
            mm = nc.tensor

            def step(t):
                up, down = t.back(UP_LAG), t.back(DOWN_LAG)
                if up.live():
                    pe.wait_ge(q_kept, up.count(1, 1))
                    for k in range(CB):
                        pe.wait_ge(scaled, up.count(CB, k + 1 - CB))
                        mm.matmul(up_bank[k][:, :], m.w_t[:, W1C + k, :], lev_t[:, :], start=True, stop=True).then_inc(uped, 1)
                if down.live():
                    pe.wait_ge(hidden, down.count(CB, CB))

                def turn_hidden(b):
                    pe.wait_ge(clipped, down.count(2 * GB, max(2 * b - 1, 0)))
                    for k in range(CB):
                        last = mm.transpose(hid_bank[:, P * k:P * k + P], hid[down.slot][:, k, S * b:S * b + S], m.id32[:, :])
                    last.then_inc(h_turned, 1)

                for b in range(GB):
                    if down.live():
                        turn_hidden(b)
                        pe.wait_ge(h_levels, down.count(GB, b + 1))
                        pe.wait_ge(l_kept, down.count(GB, b))
                        for k in range(CB):
                            last = mm.transpose(level_bank[:, 64 * k:64 * k + 64].bitcast(F16), lev2[b % 2][:, P * k:P * k + P], m.id16[:, :])
                        last.then_inc(l_turned, 1)
                        pe.wait_ge(l_kept, down.count(GB, b + 1))
                        pe.wait_ge(added, down.count(GB, b))
                        for k in range(CB):
                            last = mm.matmul(down_bank[:, 0:D], lev2_t[b % 2][:, k, :], m.w_t[:, W2C + k, :], start=k == 0, stop=k == CB - 1)
                        last.then_inc(downed, 1)
                if t.live():
                    pe.wait_ge(by_token, t.count(1, 1))
                    pe.wait_ge(r_kept, t.count(1))
                    for b in range(GB):
                        last = mm.transpose(head_bank[:, 64 * b:64 * b + 64].bitcast(F16), lev[:, b, :], m.id16[:, :])
                    last.then_inc(q_turned, 1)
                    pe.wait_ge(q_kept, t.count(1, 1))
                    for b in range(GB):
                        last = mm.matmul(head_bank[:, S * b:S * b + S], back[t.slot][:, b:b + 1].to_broadcast([P, P]), m.id32[:, :],
                                         start=True, stop=True)
                    last.then_inc(r_spread, 1)

            pipeline(pe, SPAN, NG, DOWN_LAG, step)


def program(nc, a, out, until=4):
    with ExitStack() as st:
        def sem(name):
            return st.enter_context(nc.semaphore(name))

        def sb(name, shape, dt=F32):
            return st.enter_context(nc.sbuf_tensor(name, shape, dt))

        m = Memory()
        m.bank = [st.enter_context(nc.psum_tensor(f"bank{i}", [P, 512], F32)) for i in range(8)]
        m.x = sb("x_res", [P, B, D])
        m.x_in = sem("x_in")
        m.wq = [sb("wq0", [D, D]), sb("wq1", [D, D])]
        m.wk = [sb("wk0", [D, DH]), sb("wk1", [D, D])]
        m.wv = [sb("wv0", [D, DH]), sb("wv1", [D, D])]
        m.wo = [sb("wo0", [D, D]), sb("wo1", [D, D])]
        m.qkb, m.bv, m.bo = sb("qkb", [D, 2]), sb("bv", [D, 1]), sb("bo", [P, D])
        m.rw, m.gamma, m.beta = sb("rw", [D, E]), sb("gamma", [P, D]), sb("beta", [P, D])
        m.cw, m.cb = sb("cw", [P, CB, 3]), sb("cb", [P, CB])
        m.w_t = sb("w_t", [P, NW, P], F16)
        m.s1, m.s2, m.sc = sb("s1", [P, (E + 1) * FB]), sb("s2", [P, E + 1]), sb("sc", [P, 2])
        m.s1_own, m.s2_own = sb("s1_own", [P, FB]), sb("s2_own", [P, 1])
        m.s1_t, m.s2_t = sb("s1_t", [P, FB, P]), sb("s2_t", [P, P])
        m.o_t32, m.o_t16 = sb("o_t32", [P, GT]), sb("o_t16", [P, GT], F16)
        m.id32, m.id16, m.ones = sb("id32", [P, P]), sb("id16", [P, P], F16), sb("ones", [P, P])
        m.minus_half, m.quarter, m.per_d, m.eps = (sb(x, [P, GB]) for x in ("minus_half", "quarter", "per_d", "eps"))
        m.rank = sb("rank", [P, E])
        m.pick = sb("pick", [P, E, P], F16)
        m.band_q, m.band_k, m.plain_k = sb("band_q", [P, 2, S // 2], F16), sb("band_k", [P, 2, S], F16), sb("plain_k", [P, S], F16)

        setup(nc, m, a, sem)
        if until >= 1:
            attention(nc, m, a, sem, 0)
        if until >= 2:
            expert_ffn(nc, m, a, sem)
        if until >= 3:
            attention(nc, m, a, sem, 1)
        if until >= 4:
            conv_ffn(nc, m, a, sem, out)
        else:
            left = sem("left")
            with nc.Block() as block:
                @block.sync
                def _(sp):
                    sp.wait_ge(m.x_in, 16 * NG)
                    sp.dma_start(out.rearrange("b p d -> p b d"), m.x[:, :, :]).then_inc(left, 16)
                    sp.wait_ge(left, 16)


def laid_out(inputs):
    import numpy as np

    by_dim = np.arange(D).reshape(H, DH).T.reshape(-1)
    get = {k: np.asarray(v) for k, v in inputs.items()}
    wkv = get["L0_xattn_w_kv"]
    arrays = {
        "x": get["x"], "ctx": get["ctx_1024"],
        "wq0": get["L0_xattn_w_q"][:, by_dim], "wk0": wkv[:, :DH], "wv0": wkv[:, DH:], "wo0": get["L0_xattn_w_o"],
        "wq1": get["L1_xattn_Wq"].T[:, by_dim], "wk1": get["L1_xattn_Wk"].T[:, by_dim],
        "wv1": get["L1_xattn_Wv"].T, "wo1": get["L1_xattn_Wo"].T,
        "bqk": np.stack([get["L1_xattn_bq"][by_dim], get["L1_xattn_bk"][by_dim]], 1),
        "bv": get["L1_xattn_bv"][:, None], "bo": get["L1_xattn_bo"][None, :],
        "w1s": get["L0_ffn_shared_w1"], "w2s": get["L0_ffn_shared_w2"],
        "w1e": get["L0_ffn_expert_w1"], "w2e": get["L0_ffn_expert_w2"],
        "rw": get["L0_ffn_router_w"].T, "gamma": get["L0_ffn_ln_gamma"][None, :], "beta": get["L0_ffn_ln_beta"][None, :],
        "w1c": get["L1_ffn_w1"], "w2c": get["L1_ffn_w2"],
        "cw": get["L1_ffn_conv_w"].reshape(CB, P, 3).transpose(1, 0, 2), "cb": get["L1_ffn_conv_b"].reshape(CB, P).T,
    }
    return {k: np.ascontiguousarray(v) for k, v in arrays.items()}


def kernel(**inputs):
    import concourse.bacc as bacc
    from concourse.bass_utils import run_bass_kernel_spmd

    arrays = laid_out(inputs)
    nc = bacc.Bacc("TRN2", target_bir_lowering=False, num_devices=1)
    a = {k: nc.dram_tensor(f"in_{k}", v.shape, mybir.dt.from_np(v.dtype), kind="ExternalInput").ap() for k, v in arrays.items()}
    out = nc.dram_tensor("out_x", (B, S, D), F32, kind="ExternalOutput").ap()
    program(nc, a, out)
    r = run_bass_kernel_spmd(nc, [{f"in_{k}": v for k, v in arrays.items()}], core_ids=[0])
    return r.results[0]["out_x"]
```

```python
import math
from contextlib import ExitStack

import concourse.bass as bass
from concourse import mybir

F32 = mybir.dt.float32
F16 = mybir.dt.float16
ALU = mybir.AluOpType
ACT = mybir.ActivationFunctionType
AX = mybir.AxisListType

P = 128
B = 32
S = 128
D = 128
H = 16
DH = D // H
GB = 4
NG = B // GB
GT = GB * S
WINDOW = 32
E = 8
EF = 256
FB = EF // P
CF = 512
CB = CF // P
EPS = 1e-5
SPLIT = 64.0
S2 = SPLIT * SPLIT
MASK = 60000.0
NM = P - 1
TERMS = 4
UP, LOW = TERMS * DH, 96
ROUND = 12582912.0
VM = 32
VW = DH + 1

W1E, W1S, W2E, W2S, W1C, W2C = 0, E * FB, (E + 1) * FB, (2 * E + 1) * FB, 2 * (E + 1) * FB, 2 * (E + 1) * FB + CB
NW = W2C + CB


class At:

    def __init__(self, i, off, span, size):
        self.i, self.off, self.span, self.size = i, off, span, size

    def back(self, lag):
        return At(self.i, self.off - lag, self.span, self.size)

    def live(self):
        return not isinstance(self.i, int) or 0 <= self.span * self.i + self.off < self.size

    def count(self, per, extra=0):
        value = self.i * (self.span * per) + (self.off * per + extra)
        return max(value, 0) if isinstance(value, int) else value

    def group(self):
        return At(self.i, self.off // GB, self.span // GB, self.size // GB)

    def arrivals(self, per):
        return self.i * (self.span // 2 * per) + (self.off // 2 + 1) * per

    @property
    def slot(self):
        return self.off % 2


def pipeline(eng, span, size, lag, step):
    assert lag <= span and size % span == 0
    for j in range(span):
        step(At(0, j, span, size))
    with eng.Fori(1, size // span) as i:
        for j in range(span):
            step(At(i, j, span, size))
    for j in range(lag):
        step(At(size // span, j, span, size))


class Memory:
    pass


class Chain:

    def __init__(self, eng, sem, strict=False):
        self.eng, self.sem, self.strict, self.n = eng, sem, strict, 0

    def then(self, ins):
        self.n += 1
        ins.then_inc(self.sem, 1)
        if self.strict:
            self.last()

    def last(self):
        self.eng.wait_ge(self.sem, self.n)


def setup(nc, m, a, sem):
    small_in = sem("small_weights_loaded")
    ffn_in = sem("ffn_weights_loaded")
    pool_made = sem("pool_constants")
    dve_made = sem("dve_setup_steps")
    act_made = sem("act_setup_steps")
    ternary = sem("ternary_ready")
    transposed = sem("weights_transposed")
    kept = sem("transposed_weights_kept")
    projected = sem("constants_projected")
    w_scaled, w_scaled_act, w_clipped = sem("weights_scaled"), sem("weights_scaled_act"), sem("weights_clipped")
    first_in = sem("expert_weights_loaded")
    with nc.sbuf_tensor("w_nat", [P, NW, P], F32) as w_nat, nc.sbuf_tensor("tern", [P, NW, P], F16) as tern, \
            nc.sbuf_tensor("abs_sum", [P, NW], F32) as abs_sum, nc.sbuf_tensor("inv", [P, NW], F32) as inv, \
            nc.sbuf_tensor("scale_rows", [P, 3, 16], F32) as scale_rows, \
            nc.sbuf_tensor("part_sums", [P, 2], F32) as part_sums, nc.Block() as block:
        small = [(m.wq[0], a["wq0"]), (m.wk[0], a["wk0"]), (m.wv[0], a["wv0"]), (m.wo[0], a["wo0"]), (m.wq[1], a["wq1"]),
                 (m.wk[1], a["wk1"]), (m.wv[1], a["wv1"]), (m.wo[1], a["wo1"]), (m.rw, a["rw"]),
                 (m.qkb, a["bqk"]), (m.gb, a["gb"]), (m.bv, a["bv"]), (m.cw, a["cw"]), (m.cb, a["cb"])]
        rows = [(m.bo, a["bo"])]
        CHUNKS = NW // 4
        INVERTED = 16

        def chunk(k):
            return w_nat[:, 4 * k:4 * k + 4, :]

        @block.sync
        def _(sp):
            big = [(w_nat[:, W1E:W1S, :], a["w1e"].rearrange("e (f p) d -> p (e f) d", p=P)),
                   (w_nat[:, W1S:W2E, :], a["w1s"].rearrange("(f p) d -> p f d", p=P)),
                   (w_nat[:, W2E:W2S, :].rearrange("p (e f) d -> p e (f d)", e=E), a["w2e"].rearrange("e p f -> p e f")),
                   (w_nat[:, W2S:W1C, :].rearrange("p f d -> p (f d)"), a["w2s"]),
                   (w_nat[:, W1C:W2C, :], a["w1c"].rearrange("(f p) d -> p f d", p=P)),
                   (w_nat[:, W2C:NW, :].rearrange("p f d -> p (f d)"), a["w2c"])]
            for k, (dst, src) in enumerate(big):
                sp.dma_start(dst, src).then_inc(ffn_in if k else first_in, 16)
            for g in range(NG):
                sp.dma_start(m.x[:, GB * g:GB * g + GB, :],
                             a["x"][GB * g:GB * g + GB].rearrange("b p d -> p b d")).then_inc(m.x_in, 16)

        @block.scalar
        def _(act):
            for dst, src in small:
                act.dma_start(dst[tuple(slice(None) for _ in dst.shape)], src).then_inc(small_in, 16)
            for dst, src in rows:
                act.dma_start(dst[:, :], src.to_broadcast([P, D])).then_inc(small_in, 16)
            def scale(k):
                if k < CHUNKS:
                    for w in range(4 * k, 4 * k + 4):
                        last = nc.scalar.activation(w_nat[:, w, :], w_nat[:, w, :], ACT.Copy, scale=inv[:, w:w + 1])
                    last.then_inc(w_scaled_act, 1)

            act.wait_ge(ffn_in, 5 * 16)
            act.wait_ge(first_in, 16)
            act.wait_ge(dve_made, INVERTED)
            scale(1)
            for k in range(CHUNKS):
                if k % 2 == 1:
                    scale(k + 2)
                act.wait_ge(transposed, k + 1)
                nc.scalar.activation(m.w_t[:, 4 * k:4 * k + 4, :].rearrange("p w d -> p (w d)"),
                                     m.bank[k % 2][:, 0:256].bitcast(F16), ACT.Copy).then_inc(kept, 1)
            act.wait_ge(projected, 2)
            act.wait_ge(dve_made, 1)
            nc.scalar.activation(m.s1_t[0:16, :, :].rearrange("p f d -> p (f d)"), m.bank[3][0:16, 0:256], ACT.Copy,
                                 scale=0.5).then_inc(act_made, 1)
            nc.scalar.activation(m.s2_t[0:16, :], m.bank[3][0:16, 256:384], ACT.Copy, scale=1.0 / SPLIT).then_inc(act_made, 1)

        @block.gpsimd
        def _(pl):
            g = nc.gpsimd
            step = Chain(pl, pool_made, strict=True)
            step.then(g.memset(m.id32[:, :], 0.0))
            step.then(g.memset(m.id16[:, :], 0.0))
            for t in (m.id32, m.id16):
                step.then(g.affine_select(out=t[:, :], in_=t[:, :], compare_op=ALU.not_equal, fill=1.0, base=0,
                                          pattern=[[-1, P]], channel_multiplier=1))
            for t, value in ((m.minus_half, -0.5), (m.quarter, D / 4), (m.per_d, 1.0 / D), (m.eps, EPS), (m.round, ROUND)):
                step.then(g.memset(t[:, :], value))
            step.then(g.memset(m.ones[:, :], 1.0))
            step.then(g.memset(m.pick[:, :, :], 0.0))
            for e in range(E):
                step.then(g.memset(m.rank[:, e:e + 1], float(E - e)))
            step.then(g.memset(m.band_q[:, :, :], MASK))
            step.then(g.memset(m.band_k[:, :, :], -MASK))
            step.then(g.memset(m.plain_k[:, :], 0.0))
            step.then(g.memset(m.gather[:, :, :], 0.0))
            for base in (0, -VW):
                step.then(g.affine_select(out=m.gather[:, :, :], in_=m.gather[:, :, :], compare_op=ALU.not_equal, fill=1.0,
                                          base=base, pattern=[[-VM, 4], [-1, VW]], channel_multiplier=1))
            for layer, per in enumerate((1.0, DH ** -0.5)):
                step.then(g.memset(m.shift[:, layer:layer + 1], math.log(SPLIT) / per))
            step.then(g.affine_select(out=m.pick[:, :, :], in_=m.pick[:, :, :], compare_op=ALU.not_equal, fill=1.0,
                                      base=0, pattern=[[-1, E], [0, P]], channel_multiplier=1))
            for half in range(2):
                q0, dq, k0, dk = (0, 1, 0, 1) if half == 0 else (63, -1, S - 1, -1)
                for lo_p, hi_p, tile, base, step_x, mult in (
                        (0, LOW, m.band_q, -UP - q0, -dq, 1), (0, LOW, m.band_k, k0 + UP - WINDOW - 1, dk, -1),
                        (LOW, P, m.band_q, q0 - WINDOW - 1, dq, -1), (LOW, P, m.band_k, -k0, -dk, 1)):
                    part = tile[lo_p:hi_p, half, :]
                    step.then(g.affine_select(out=part, in_=part, compare_op=ALU.is_ge, fill=0.0, base=base,
                                              pattern=[[step_x, part.shape[-1]]], channel_multiplier=mult))
            for tile, fill, first in ((m.band_q, 0.0, LOW), (m.band_k, S2, LOW), (m.plain_k, S2, 0)):
                part = tile[first:P]
                part = part.rearrange("p a b -> p (a b)") if len(tile.shape) == 3 else part
                step.then(g.affine_select(out=part, in_=part, compare_op=ALU.is_gt, fill=fill, base=NM - first,
                                          pattern=[[0, part.shape[-1]]], channel_multiplier=-1))

        @block.vector
        def _(dve):
            v = nc.vector
            step = Chain(dve, dve_made)
            for t in (m.s1_t, m.s2_t, m.o_t32, m.o_t16, scale_rows):
                last = v.memset(t[tuple(slice(None) for _ in t.shape)], 0.0)
            step.then(last)
            dve.wait_ge(first_in, 16)
            v.tensor_reduce(abs_sum[:, 0:W1S], w_nat[:, 0:W1S, :], AX.X, ALU.add, apply_absolute_value=True)
            dve.wait_ge(ffn_in, 5 * 16)
            step.last()
            step.then(v.tensor_reduce(abs_sum[:, W1S:], w_nat[:, W1S:, :], AX.X, ALU.add, apply_absolute_value=True))
            step.last()
            step.then(v.tensor_scalar(m.s1[:, :], abs_sum[:, W1E:W2E], 1.0 / D, EPS, ALU.mult, ALU.max))
            pairs = abs_sum[:, W2E:W1C].rearrange("p (e f) -> p f e", f=FB)
            step.then(v.tensor_tensor(m.s2[:, :], pairs[:, 0, :], pairs[:, 1, :], ALU.add))
            for k, at in enumerate((W1C, W2C)):
                step.then(v.tensor_reduce(part_sums[:, k:k + 1], abs_sum[:, at:at + CB], AX.X, ALU.add))
            step.last()
            sums_ready = step.n
            step.then(v.tensor_scalar(m.s2[:, :], m.s2[:, :], 1.0 / EF, EPS, ALU.mult, ALU.max))
            step.last()
            step.then(v.reciprocal(inv[:, W1E:W2E], m.s1[:, :]))
            step.then(v.reciprocal(inv[:, W2E:W1C:2], m.s2[:, :]))
            step.then(v.reciprocal(inv[:, W2E + 1:W1C:2], m.s2[:, :]))
            step.then(v.tensor_copy(scale_rows[:, 0:FB, 0:E], m.s1[:, 0:E * FB].rearrange("p (e f) -> p f e", f=FB)))
            step.then(v.tensor_copy(scale_rows[:, FB, E:2 * E], m.s2[:, 0:E]))
            assert sums_ready == 6 and step.n == 12
            dve.wait_ge(projected, 1)
            step.then(v.tensor_scalar(m.sc[:, :], m.bank[2][:, 0:2], 1.0 / (CF * D), EPS, ALU.mult, ALU.max))
            step.last()
            step.then(v.reciprocal(part_sums[:, :], m.sc[:, :]))
            step.last()
            for k, at in enumerate((W1C, W2C)):
                step.then(v.tensor_copy(inv[:, at:at + CB], part_sums[:, k:k + 1].to_broadcast([P, CB])))
            assert step.n == INVERTED
            step.last()
            for k in range(CHUNKS + 2):
                if k < CHUNKS and k % 2 == 0:
                    v.tensor_tensor(chunk(k), chunk(k), inv[:, 4 * k:4 * k + 4].unsqueeze(2).to_broadcast([P, 4, P]), ALU.mult
                                    ).then_inc(w_scaled, 1)
                if 1 <= k <= CHUNKS:
                    c = k - 1
                    dve.wait_ge((w_scaled, w_scaled_act)[c % 2], c // 2 + 1)
                    v.tensor_scalar(chunk(c), chunk(c), -1.0, 1.0, ALU.max, ALU.min).then_inc(w_clipped, 1)
                if k >= 2:
                    dve.wait_ge(w_clipped, k - 1)
                    v.tensor_scalar(tern[:, 4 * k - 8:4 * k - 4, :], chunk(k - 2), ROUND, -ROUND, ALU.add, ALU.add).then_inc(ternary, 1)
            dve.wait_ge(small_in, (len(small) + len(rows)) * 16)
            step.then(v.tensor_scalar(m.qkb[:, :], m.qkb[:, :], SPLIT, None, ALU.mult))
            step.then(v.tensor_scalar(m.gb[:, :], m.gb[:, :], SPLIT, None, ALU.mult))
            step.then(v.tensor_scalar(m.cw[:, :, :], m.cw[:, :, :], 0.5, None, ALU.mult))
            step.then(v.tensor_scalar(m.cb[:, :], m.cb[:, :], 0.5, None, ALU.mult))
            step.then(v.tensor_scalar(m.s1_own[:, :], m.s1[:, E * FB:], 0.5, None, ALU.mult))
            step.then(v.tensor_scalar(m.s2_own[:, :], m.s2[:, E:], 1.0 / SPLIT, None, ALU.mult))
            dve.wait_ge(projected, 3)
            step.then(v.tensor_tensor(m.bo[:, :], m.bank[4][:, 0:D], m.bo[:, :], ALU.add))

        @block.tensor
        def _(pe):
            t = nc.tensor
            pe.wait_ge(pool_made, 10)
            pe.wait_ge(dve_made, 6)
            t.matmul(m.bank[2][:, 0:2], m.ones[:, :], part_sums[:, :], start=True, stop=True).then_inc(projected, 1)
            pe.wait_ge(dve_made, 12)
            for k in range(3):
                last = t.matmul(m.bank[3][0:16, P * k:P * k + P], scale_rows[:, k, :], m.id32[:, :], start=True, stop=True,
                                is_transpose=True)
            last.then_inc(projected, 1)
            pe.wait_ge(small_in, (len(small) + len(rows)) * 16)
            t.matmul(m.bank[4][:, 0:D], m.bv[:, :].to_broadcast([P, P]), m.wo[1][:, :], start=True, stop=True).then_inc(projected, 1)
            for k in range(CHUNKS):
                pe.wait_ge(ternary, k + 1)
                if k >= 2:
                    pe.wait_ge(kept, k - 1)
                for w in range(4):
                    last = t.transpose(m.bank[k % 2][:, 64 * w:64 * w + 64].bitcast(F16), tern[:, 4 * k + w, :], m.id16[:, :])
                last.then_inc(transposed, 1)


class Norm:

    def __init__(self, nc, st, sem, n, twice=False):
        self.twice, self.moments = twice, 14 if twice else 9
        self.bn = st.enter_context(nc.sbuf_tensor(n + "bn", [P, GB, 6], F32))
        self.mean, self.rs, self.apart, self.pooled = (st.enter_context(nc.sbuf_tensor(n + x, [P, GB], F32))
                                                       for x in ("mean", "rs", "apart", "pooled"))
        self.stats, self.moment, self.normed = (sem(n + x) for x in ("stats", "moment", "normed"))


def norm_stats(nc, dve, f, g, rows):
    dve.wait_ge(f.moment, g.count(f.moments))
    for b in range(GB):
        last = nc.vector.bn_stats(f.bn[:, b, :], rows(b))
    last.then_inc(f.stats, 1)


def norm_rstd(nc, m, pl, f, g):
    gp = nc.gpsimd
    even_mean, even_m2, odd_mean, odd_m2 = (f.bn[:, :, k] for k in (1, 2, 4, 5))

    def after(k):
        pl.wait_ge(f.moment, g.count(f.moments, k))

    pl.wait_ge(f.stats, g.count(1, 1))
    pl.wait_ge(f.normed, g.count(1))
    gp.tensor_tensor(out=f.mean[:, :], in0=even_mean, in1=odd_mean, op=ALU.add).then_inc(f.moment, 1)
    gp.tensor_tensor(out=f.apart[:, :], in0=even_mean, in1=odd_mean, op=ALU.subtract).then_inc(f.moment, 1)
    gp.tensor_tensor(out=f.pooled[:, :], in0=even_m2, in1=odd_m2, op=ALU.add).then_inc(f.moment, 1)
    after(3)
    gp.tensor_tensor(out=f.apart[:, :], in0=f.apart[:, :], in1=f.apart[:, :], op=ALU.mult)
    gp.tensor_scalar(f.mean[:, :], f.mean[:, :], 0.5, None, ALU.mult).then_inc(f.moment, 1)
    after(4)
    gp.tensor_tensor(out=f.apart[:, :], in0=f.apart[:, :], in1=m.quarter[:, :], op=ALU.mult).then_inc(f.moment, 1)
    after(5)
    gp.tensor_tensor(out=f.pooled[:, :], in0=f.pooled[:, :], in1=f.apart[:, :], op=ALU.add).then_inc(f.moment, 1)
    after(6)
    gp.tensor_tensor(out=f.apart[:, :], in0=f.pooled[:, :], in1=m.per_d[:, :], op=ALU.mult).then_inc(f.moment, 1)
    after(7)
    gp.tensor_tensor(out=f.pooled[:, :], in0=f.apart[:, :], in1=m.eps[:, :], op=ALU.add).then_inc(f.moment, 1)
    after(8)
    gp.tensor_tensor(out=f.rs[:, :], in0=f.pooled[:, :], in1=m.minus_half[:, :], op=ALU.pow).then_inc(f.moment, 1)
    if f.twice:
        after(9)
        gp.tensor_tensor(out=f.apart[:, :], in0=f.apart[:, :], in1=f.rs[:, :], op=ALU.mult).then_inc(f.moment, 1)
        after(10)
        gp.tensor_tensor(out=f.apart[:, :], in0=f.apart[:, :], in1=f.rs[:, :], op=ALU.mult).then_inc(f.moment, 1)
        after(11)
        gp.tensor_tensor(out=f.apart[:, :], in0=f.apart[:, :], in1=m.eps[:, :], op=ALU.add).then_inc(f.moment, 1)
        after(12)
        gp.tensor_tensor(out=f.apart[:, :], in0=f.apart[:, :], in1=m.minus_half[:, :], op=ALU.pow).then_inc(f.moment, 1)
        after(13)
        gp.tensor_tensor(out=f.rs[:, :], in0=f.rs[:, :], in1=f.apart[:, :], op=ALU.mult).then_inc(f.moment, 1)


def norm_apply(nc, dve, f, g, rows, out):
    dve.wait_ge(f.moment, g.count(f.moments, f.moments))
    for b in range(GB):
        last = nc.vector.tensor_scalar(out(b), rows(b), f.mean[:, b:b + 1], f.rs[:, b:b + 1], ALU.subtract, ALU.mult)
    last.then_inc(f.normed, 1)


def group_rows(m, g):
    first = g.i * (g.span * GB) + g.off * GB
    return lambda b: m.x[:, bass.ds(first + b, 1), :].rearrange("p b d -> p (b d)")


def attention(nc, m, a, sem, layer):
    QM_LAG, NM_LAG, KM_LAG, PV_LAG, OUT_LAG = 4, 4, 6, 7, 8
    SPAN = 2 * GB
    KG = 2 if layer == 0 else H
    KR = DH if layer == 0 else D
    VN = 1 if layer == 0 else H
    exp_scale = (1.0 if layer == 0 else DH ** -0.5) / S2
    stack_dmas = 2 * TERMS
    n = f"a{layer}_"

    def s(name):
        return sem(n + name)

    ctx_in = [s("ctx_in0"), s("ctx_in1")]
    init = s("operands_cleared")
    turned_x, turned_c, xt_kept, ct_kept = s("turned_x"), s("turned_c"), s("xt_kept"), s("ct_kept")
    q_proj, k_proj, v_proj = s("q_proj"), s("k_proj"), s("v_proj")
    q_hi, k_hi, q_lo, k_lo, v_kept = s("q_hi"), s("k_hi"), s("q_lo"), s("k_lo"), s("v_kept")
    stacked, biased = s("stacked"), s("biased")
    by_query, maxed = s("scores_by_query"), s("maxed")
    max_turned, max_kept, max_in = s("max_turned"), s("max_kept"), [s("max_in0"), s("max_in1")]
    by_key = s("scores_by_key")
    prob_hi, prob_lo_dve, prob_lo_pool = s("prob_hi_ready"), s("prob_lo_dve"), s("prob_lo_pool")
    weighted, wv_kept, gathered = s("weighted"), s("weighted_kept"), s("gathered")
    recip, o_ready = s("recip"), s("o_ready")
    o_turned, ot_kept, out_proj, added = s("o_turned"), s("ot_kept"), s("out_proj"), s("added")
    v_hi = s("v_hi")

    with ExitStack() as st:
        def sb(name, shape, dt=F32):
            return st.enter_context(nc.sbuf_tensor(n + name, shape, dt))

        ctx_tok = [sb(f"ctx_tok{i}", [P, GB, D]) for i in range(2)]
        norm = Norm(nc, st, sem, n)
        xn = sb("xn", [P, GB, D])
        x_t = sb("x_t", [P, GT])
        c_t = sb("c_t", [P, GT])
        qk = sb("qk", [P, 2, GT])
        hi = sb("hi", [P, 2, GT], F16)
        lo = sb("lo", [P, 2, GT], F16)
        qs = [sb(f"qs{i}", [P, H, GT], F16) for i in range(2)]
        ks = [sb(f"ks{i}", [P, KG, GT], F16) for i in range(2)]
        vs = [sb(f"vs{i}", [P, GB, VN, VM], F16) for i in range(2)]
        v32 = sb("v32", [P, GB, VN, DH])
        nmax = [sb(f"nmax{i}", [P, H]) for i in range(2)]
        nmax_t = [sb(f"nmax_t{i}", [H, S], F16) for i in range(2)]
        prob = sb("prob", [P, H, S])
        prob16 = [sb(f"prob16_{i}", [P, 2, H, S], F16) for i in range(2)]
        wv = sb("wv", [P, 4, S])
        rec = [sb(f"rec{i}", [P, H]) for i in range(2)]
        o_tok = [sb(f"o_tok{i}", [P, D]) for i in range(2)]
        o_t = sb("o_t", [P, S])
        block = st.enter_context(nc.Block())

        query_bank, key_bank = m.bank[0:2], m.bank[2:4]
        turn_bank, out_bank, x_bank, c_bank = m.bank[4:8]
        by_q = out_bank[:, 0:H * VW].rearrange("p (g w) -> p g w", g=H)
        o_turn, o_proj = out_bank[:, 144:144 + S], out_bank[:, 272:272 + D]

        def prob_lower(eng, engine, t, u, done):
            if t.live():
                eng.wait_ge(prob_hi, t.count(4, 2 * (u // 2) + 2 if layer == 0 else u + 1))
                hs = slice(4 * u, 4 * u + 4)
                engine.tensor_tensor(out=prob16[t.slot][:, 1, hs, :], in0=prob[:, hs, :], in1=prob16[t.slot][:, 0, hs, :],
                                     op=ALU.subtract).then_inc(done, 1)

        @block.sync
        def _(sp):
            def step(t):
                g = t.group()
                if t.live() and t.off % GB == 0:
                    first = g.i * (2 * GB) + g.off * GB
                    first = first if isinstance(first, int) else sp.snap(first)
                    sp.wait_ge(turned_c, g.count(1, -1))
                    sp.dma_start(ctx_tok[g.slot][:, :, :], a["ctx"][bass.ds(first, GB), :, :].rearrange("b p d -> p b d")
                                 ).then_inc(ctx_in[g.slot], 16)
                if t.live() and t.off % GB == 2:
                    if isinstance(g.i, int):
                        sp.wait_ge(init, 3 + g.slot)
                    sp.wait_ge(q_lo, g.count(1, 1))
                    for term in range(TERMS):
                        sp.dma_start(qs[g.slot][DH * term:DH * term + DH, :, :],
                                     (hi, hi, lo, lo)[term][:, 0, :]).then_inc(stacked, 16)
                if t.live() and t.off % GB == 3:
                    sp.wait_ge(k_lo, g.count(1, 1))
                    for term in range(TERMS):
                        half = (hi, lo, hi, lo)[term]
                        sp.dma_start(ks[g.slot][DH * term:DH * term + DH, :, :],
                                     half[:, 1, :] if layer == 1 else half[0:DH, 1, :].unsqueeze(1).to_broadcast([DH, KG, GT])
                                     ).then_inc(stacked, 16)
                u = t.back(NM_LAG)
                if u.live():
                    sp.wait_ge(max_kept, u.count(1, 1))
                    b0 = u.off % GB * S
                    row = qs[u.group().slot][NM:P, :, b0:b0 + S]
                    sp.dma_start(row, nmax_t[u.slot][:, :]).then_inc(max_in[u.slot], 16)

            pipeline(sp, SPAN, B, OUT_LAG, step)

        @block.gpsimd
        def _(pl):
            g_ = nc.gpsimd

            def step(t):
                g = t.group()
                if t.live() and t.off % GB == 0:
                    norm_rstd(nc, m, pl, norm, g)
                km = t.back(KM_LAG)
                prob_lower(pl, g_, km, 1, prob_lo_pool)
                prob_lower(pl, g_, km, 3, prob_lo_pool)
                if layer == 1 and t.live() and t.off % GB == 0:
                    pl.wait_ge(norm.normed, g.count(1, 1))
                    xg = m.x[:, bass.ds(g.i * (2 * GB) + g.off * GB, GB), :]
                    g_.tensor_tensor(out=xg, in0=xg, in1=m.bo[:, :].unsqueeze(1).to_broadcast([P, GB, D]),
                                     op=ALU.add).then_inc(biased, 1)

            pipeline(pl, SPAN, B, OUT_LAG, step)

        @block.scalar
        def _(act):
            f = nc.scalar

            def copy(out, in_, func=ACT.Copy, **more):
                return f.activation(out, in_, func, **more)

            def exp(t, u):
                if not t.live():
                    return
                if u == 0:
                    act.wait_ge(weighted, t.count(1, -1))
                if u % 2 == 0:
                    act.wait_ge(prob_lo_dve, t.count(2, u // 2 - 1))
                    act.wait_ge(prob_lo_pool, t.count(2, u // 2 - 1))
                act.wait_ge(by_key, t.count(4, u + 1))
                for dst in (prob, prob16[t.slot][:, 0]):
                    if layer == 0:
                        half, h0 = u % 2, 8 * (u // 2)
                        dst = dst[:, h0:h0 + 8, 64 * half:64 * half + 64]
                        src = key_bank[u % 2][:, :].rearrange("p (h s) -> p h s", h=8)
                    else:
                        dst = dst[:, 4 * u:4 * u + 4, :].rearrange("p h s -> p (h s)")
                        src = key_bank[u % 2][:, :]
                    last = copy(dst, src, ACT.Exp, scale=exp_scale)
                last.then_inc(prob_hi, 1)

            def step(t):
                g = t.group()
                km, nm, out = t.back(KM_LAG), t.back(NM_LAG), t.back(OUT_LAG)
                if out.live():
                    act.wait_ge(weighted, out.count(1, 1))
                    act.wait_ge(gathered, out.count(1))
                    copy(wv[:, :, :].rearrange("p j s -> p (j s)"), out_bank[:, :]).then_inc(wv_kept, 1)
                exp(km, 0)
                exp(km, 1)
                if t.live() and t.off % GB == 1:
                    act.wait_ge(turned_x, g.count(1, 1))
                    copy(x_t[:, :], x_bank[:, :]).then_inc(xt_kept, 1)
                exp(km, 2)
                if out.live():
                    act.wait_ge(o_turned, out.count(1, 1))
                    copy(o_t[:, :], o_turn).then_inc(ot_kept, 1)
                exp(km, 3)
                if t.live() and t.off % GB == 0:
                    act.wait_ge(turned_c, g.count(1, 1))
                    copy(c_t[:, :], c_bank[:, :]).then_inc(ct_kept, 1)
                if t.live() and t.off % GB in (1, 2):
                    k = t.off % GB - 1
                    rows, proj, bank, split = ((D, q_proj, x_bank, q_hi), (KR, k_proj, c_bank, k_hi))[k]
                    act.wait_ge(stacked, g.count(16 * stack_dmas))
                    act.wait_ge((q_lo, k_lo)[k], g.count(1))
                    act.wait_ge(proj, g.count(1, 1))
                    if layer == 0:
                        copy(qk[0:rows, k, :], bank[0:rows, :], scale=SPLIT)
                        copy(hi[0:rows, k, :], bank[0:rows, :], scale=SPLIT).then_inc(split, 1)
                    else:
                        copy(qk[:, k, :], bank[:, :], ACT.Identity, scale=SPLIT, bias=m.qkb[:, k:k + 1])
                        copy(hi[:, k, :], bank[:, :], ACT.Identity, scale=SPLIT, bias=m.qkb[:, k:k + 1]).then_inc(split, 1)
                if t.live() and t.off % GB == 3:
                    if isinstance(g.i, int) and g.off == 0:
                        act.wait_ge(init, 2)
                    act.wait_ge(v_proj, g.count(1, 1))
                    act.wait_ge(weighted, g.count(GB, -GB))
                    act.wait_ge(v_kept, g.count(1))
                    src = c_bank[:, 0:GB * VN * DH].rearrange("p (b h d) -> p b h d", b=GB, h=VN)
                    copy(v32[:, :, :, :], src, scale=SPLIT)
                    copy(vs[g.slot][:, :, :, 0:DH], src, scale=SPLIT).then_inc(v_hi, 1)
                if nm.live():
                    act.wait_ge(max_turned, nm.count(1, 1))
                    act.wait_ge(max_in[nm.slot], nm.arrivals(16) - 16)
                    copy(nmax_t[nm.slot][:, :], turn_bank[0:H, 0:S], ACT.Identity, scale=1.0 / S2, bias=m.shift[0:H, layer:layer + 1]
                         ).then_inc(max_kept, 1)

            pipeline(act, SPAN, B, OUT_LAG, step)

        @block.vector
        def _(dve):
            v = nc.vector

            def row_max(t, u):
                if not t.live():
                    return
                dve.wait_ge(by_query, t.count(4, u + 1))
                if u == 0:
                    dve.wait_ge(max_turned, t.count(1, -1))
                dst = nmax[t.slot][:, 4 * u:4 * u + 4]
                src = query_bank[u % 2][:, :].rearrange("p (h k) -> p h k", h=4)
                v.tensor_reduce(dst, src, AX.X, ALU.max, negate=True).then_inc(maxed, 1)

            def clear_values():
                for i in range(2):
                    last = v.memset(vs[i][:, :, :, :].rearrange("p b h w -> p (b h w)"), 0.0)
                last.then_inc(init, 1)
                dve.wait_ge(init, 1)
                for i in range(2):
                    last = v.memset(vs[i][:, :, :, DH:VW], SPLIT)
                last.then_inc(init, 1)

            def clear_scores(i):
                v.tensor_copy(qs[i][:, :, :].rearrange("p h (b s) -> p (h b) s", b=GB),
                              m.band_q[:, :, :].rearrange("p f s -> p (f s)").unsqueeze(1).to_broadcast([P, H * GB, S]))
                if layer == 0:
                    last = v.tensor_copy(ks[i][:, :, :].rearrange("p f (b s) -> p f b s", b=GB),
                                         m.band_k[:, :, :].unsqueeze(2).to_broadcast([P, 2, GB, S]))
                else:
                    last = v.tensor_copy(ks[i][:, :, :].rearrange("p h (b s) -> p (h b) s", b=GB),
                                         m.plain_k[:, :].unsqueeze(1).to_broadcast([P, H * GB, S]))
                last.then_inc(init, 1)

            def step(t):
                g = t.group()
                qm, km, out = t.back(QM_LAG), t.back(KM_LAG), t.back(OUT_LAG)
                front = t.live() and t.off % GB == 0
                rows = group_rows(m, g)
                if front:
                    if layer == 0 and isinstance(g.i, int) and g.off == 0:
                        dve.wait_ge(m.x_in, 16 * NG)
                    norm_stats(nc, dve, norm, g, rows)
                    if isinstance(g.i, int) and g.off == 0:
                        clear_values()
                        clear_scores(0)
                if isinstance(t.i, int) and t.i == 0 and t.off == 1:
                    clear_scores(1)
                row_max(qm, 0)
                row_max(qm, 1)
                if t.live() and t.off % GB in (2, 3):
                    k = t.off % GB - 2
                    used, split, done = ((D, q_hi, q_lo), (KR, k_hi, k_lo))[k]
                    dve.wait_ge(split, g.count(1, 1))
                    v.tensor_tensor(lo[0:used, k, :], qk[0:used, k, :], hi[0:used, k, :], ALU.subtract).then_inc(done, 1)
                last_g = t.back(GB).group()
                if last_g.live() and t.off % GB == 0:
                    dve.wait_ge(v_hi, last_g.count(1, 1))
                    v.tensor_tensor(vs[last_g.slot][:, :, :, VW:VW + DH], v32[:, :, :, :], vs[last_g.slot][:, :, :, 0:DH],
                                    ALU.subtract).then_inc(v_kept, 1)
                if out.live():
                    dve.wait_ge(gathered, out.count(1, 1))
                    v.reciprocal(rec[out.slot][:, :], by_q[:, :, DH]).then_inc(recip, 1)
                    dve.wait_ge(o_turned, out.count(1))
                    dve.wait_ge(recip, out.count(1, 1))
                    v.tensor_tensor(o_tok[out.slot][:, :].rearrange("p (g d) -> p g d", g=H), by_q[:, :, 0:DH],
                                    rec[out.slot][:, :].unsqueeze(2).to_broadcast([P, H, DH]), ALU.mult).then_inc(o_ready, 1)
                row_max(qm, 2)
                prob_lower(dve, v, km, 0, prob_lo_dve)
                row_max(qm, 3)
                if front:
                    dve.wait_ge(turned_x, g.count(1))
                    norm_apply(nc, dve, norm, g, rows, lambda b: xn[:, b, :])
                if out.live():
                    if layer == 1:
                        dve.wait_ge(biased, out.group().count(1, 1))
                    dve.wait_ge(out_proj, out.count(1, 1))
                    xb = m.x[:, bass.ds(out.count(1), 1), :].rearrange("p b d -> p (b d)")
                    v.tensor_tensor(xb, o_proj, xb, ALU.add).then_inc(added, 1)
                prob_lower(dve, v, km, 2, prob_lo_dve)

            pipeline(dve, SPAN, B, OUT_LAG, step)

        @block.tensor
        def _(pe):
            mm = nc.tensor

            def scores_by_query(t, u):
                if not t.live():
                    return
                q, k, b0 = qs[t.group().slot], ks[t.group().slot], t.off % GB * S
                if u == 0:
                    if isinstance(t.i, int) and t.off % GB == 0:
                        pe.wait_ge(init, 3 + t.group().slot)
                    pe.wait_ge(stacked, t.group().count(16 * stack_dmas, 16 * stack_dmas))
                pe.wait_ge(maxed, t.count(4, u - 1))
                for j in range(4):
                    h, dst = 4 * u + j, query_bank[u % 2][:, S * j:S * j + S]
                    if layer == 0:
                        for half in range(2):
                            last = mm.matmul(dst[64 * half:64 * half + 64, :], q[0:NM, h, b0 + 64 * half:b0 + 64 * half + 64],
                                             k[0:NM, half, b0:b0 + S], start=True, stop=True)
                    else:
                        last = mm.matmul(dst, q[0:NM, h, b0:b0 + S], k[0:NM, h, b0:b0 + S], start=True, stop=True)
                last.then_inc(by_query, 1)

            def scores_by_key(t, u):
                if not t.live():
                    return
                q, k, b0 = qs[t.group().slot], ks[t.group().slot], t.off % GB * S
                if u == 0:
                    pe.wait_ge(max_in[t.slot], t.arrivals(16))
                pe.wait_ge(prob_hi, t.count(4, u - 1))
                if layer == 0:
                    half, h0 = u % 2, 8 * (u // 2)
                    last = mm.matmul(key_bank[u % 2][:, :], k[:, half, b0:b0 + S],
                                     q[:, h0:h0 + 8, b0 + 64 * half:b0 + 64 * half + 64], start=True, stop=True)
                else:
                    for j in range(4):
                        last = mm.matmul(key_bank[u % 2][:, S * j:S * j + S], k[:, 4 * u + j, b0:b0 + S],
                                         q[:, 4 * u + j, b0:b0 + S], start=True, stop=True)
                last.then_inc(by_key, 1)

            def step(t):
                g = t.group()
                qm, nm, km, pv, out = (t.back(lag) for lag in (QM_LAG, NM_LAG, KM_LAG, PV_LAG, OUT_LAG))
                scores_by_query(qm, 0)
                scores_by_key(km, 0)
                if t.live() and t.off % GB == 1:
                    pe.wait_ge(norm.normed, g.count(1, 1))
                    pe.wait_ge(q_hi, g.count(1))
                    for b in range(GB):
                        last = mm.transpose(x_bank[:, S * b:S * b + S], xn[:, b, :], m.id32[:, :])
                    last.then_inc(turned_x, 1)
                scores_by_query(qm, 1)
                scores_by_key(km, 1)
                if out.live():
                    pe.wait_ge(wv_kept, out.count(1, 1))
                    for j in range(4):
                        last = mm.matmul(by_q[:, 4 * j:4 * j + 4, :].rearrange("p g w -> p (g w)"), wv[:, j, :],
                                         m.gather[:, :, :].rearrange("p u w -> p (u w)"), start=True, stop=True)
                    last.then_inc(gathered, 1)
                scores_by_query(qm, 2)
                scores_by_key(km, 2)
                if t.live() and t.off % GB == 0:
                    pe.wait_ge(ctx_in[g.slot], g.arrivals(16))
                    pe.wait_ge(v_hi, g.count(1))
                    for b in range(GB):
                        last = mm.transpose(c_bank[:, S * b:S * b + S], ctx_tok[g.slot][:, b, :], m.id32[:, :])
                    last.then_inc(turned_c, 1)
                if t.live() and t.off % GB == 1:
                    pe.wait_ge(xt_kept, g.count(1, 1))
                    mm.matmul(x_bank[:, :], m.wq[layer][:, :], x_t[:, :], start=True, stop=True).then_inc(q_proj, 1)
                if t.live() and t.off % GB == 2:
                    pe.wait_ge(ct_kept, g.count(1, 1))
                    mm.matmul(c_bank[0:KR, :], m.wk[layer][:, :], c_t[:, :], start=True, stop=True).then_inc(k_proj, 1)
                if t.live() and t.off % GB == 3:
                    pe.wait_ge(k_hi, g.count(1, 1))
                    w = VN * DH
                    for b in range(GB):
                        last = mm.matmul(c_bank[:, w * b:w * b + w], c_t[:, S * b:S * b + S], m.wv[layer][:, :],
                                         start=True, stop=True)
                    last.then_inc(v_proj, 1)
                if out.live():
                    pe.wait_ge(o_ready, out.count(1, 1))
                    mm.transpose(o_turn, o_tok[out.slot][:, :], m.id32[:, :]).then_inc(o_turned, 1)
                scores_by_query(qm, 3)
                scores_by_key(km, 3)
                if out.live():
                    pe.wait_ge(ot_kept, out.count(1, 1))
                    mm.matmul(o_proj, o_t[:, :], m.wo[layer][:, :], start=True, stop=True).then_inc(out_proj, 1)
                if nm.live():
                    pe.wait_ge(max_kept, nm.count(1))
                    pe.wait_ge(maxed, nm.count(4, 4))
                    mm.transpose(turn_bank[0:H, 0:S], nmax[nm.slot][:, :], m.id32[:, :]).then_inc(max_turned, 1)
                if pv.live():
                    pg = pv.group()
                    pe.wait_ge(prob_lo_dve, pv.count(2, 2))
                    pe.wait_ge(prob_lo_pool, pv.count(2, 2))
                    if pv.off % GB == 0:
                        pe.wait_ge(v_kept, pg.count(1, 1))
                    pe.wait_ge(added, pv.count(1))
                    for u in range(4):
                        for j in range(4 if layer == 1 else 1):
                            h, n_h = 4 * u + j, 1 if layer == 1 else 4
                            for half in range(2):
                                last = mm.matmul(out_bank[VM * u:VM * u + VM, S * j:S * (j + n_h)],
                                                 vs[pg.slot][:, pv.off % GB, h % VN, :], prob16[pv.slot][:, half, h:h + n_h, :],
                                                 start=half == 0, stop=half == 1)
                    last.then_inc(weighted, 1)

            pipeline(pe, SPAN, B, OUT_LAG, step)


def expert_ffn(nc, m, a, sem):
    UP_LAG, DOWN_LAG, SPAN = 1, 2, 2
    ROUTE = 12
    GATED = (2, 3, 0, 1)
    n = "e_"

    def s(name):
        return sem(n + name)

    head_tile, head_kept, lo_ready = s("head_tile"), s("head_kept"), s("lo_ready")
    route_tile, route_kept = s("route_tile"), s("route_kept")
    router, exped, onehot = s("router"), s("exped"), s("onehot")
    masked, up_used = s("masked"), s("up_used")
    z_scaled, z_own, tanhed, gated, h1_hi, h1_lo = s("z_scaled"), s("z_own"), s("tanhed"), s("gated"), s("h1_hi"), s("h1_lo")
    gate_step = s("gate_step")
    h1_masked, down_used = s("h1_masked"), s("down_used")
    y_step, y_ready, y_turned, added = s("y_step"), s("y_ready"), s("y_turned"), s("added")

    with ExitStack() as st:
        def sb(name, shape, dt=F32):
            return st.enter_context(nc.sbuf_tensor(n + name, shape, dt))

        norm = Norm(nc, st, sem, n, twice=True)
        hn = sb("hn", [P, GB, D])
        h_t = sb("h_t", [P, GT])
        h_half = [sb(f"h_half{i}", [P, 2, GT], F16) for i in range(2)]
        logits = sb("logits", [P, GB, E])
        below = sb("below", [P, GB, E])
        ex = sb("ex", [P, GB, E])
        cand = sb("cand", [P, GB, E])
        top = sb("top", [P, 3, GB])
        choice = sb("choice", [P, GB, 2 * E])
        masks = [sb(f"masks{i}", [P, E, GT], F16) for i in range(2)]
        s1_tok = sb("s1_tok", [P, FB, GT])
        s2_tok = [sb(f"s2_tok{i}", [P, GT]) for i in range(2)]
        hm = [sb(f"hm{i}", [P, 2, GT], F16) for i in range(2)]
        z = sb("z", [P, 2 * FB, GT])
        th = sb("th", [P, 2 * FB, GT])
        h1 = [sb(f"h1{i}", [P, 2, 2 * FB, GT], F16) for i in range(2)]
        h1m = [sb(f"h1m{i}", [P, 2, GT], F16) for i in range(4)]
        routed = sb("routed", [P, GT])
        y = sb("y", [P, GT])
        block = st.enter_context(nc.Block())

        up_bank, down_bank, front_bank = m.bank[0:4], m.bank[4:6], m.bank[6:8]

        @block.gpsimd
        def _(pl):
            def step(t):
                up = t.back(UP_LAG)
                if t.live():
                    norm_rstd(nc, m, pl, norm, t)
                if up.live():
                    for k, f in enumerate(GATED[:FB]):
                        pl.wait_ge(tanhed, up.count(2 * FB, k + 1))
                        nc.gpsimd.tensor_tensor(out=th[:, f, :], in0=th[:, f, :], in1=z[:, f, :], op=ALU.mult).then_inc(gate_step, 1)
                        pl.wait_ge(gate_step, up.count(2 * FB, 2 * k + 1))
                        nc.gpsimd.tensor_tensor(out=th[:, f, :], in0=th[:, f, :], in1=z[:, f, :], op=ALU.add).then_inc(gate_step, 1)
                if t.live():
                    pl.wait_ge(head_kept, t.count(2, 1))
                    nc.gpsimd.tensor_tensor(out=h_half[t.slot][:, 1, :], in0=h_t[:, :], in1=h_half[t.slot][:, 0, :], op=ALU.subtract
                                            ).then_inc(lo_ready, 1)
                if up.live():
                    for k, f in enumerate(GATED):
                        pl.wait_ge(h1_hi, up.count(2 * FB, k + 1))
                        nc.gpsimd.tensor_tensor(out=h1[up.slot][:, 1, f, :], in0=th[:, f, :], in1=h1[up.slot][:, 0, f, :],
                                                op=ALU.subtract).then_inc(h1_lo, 1)

            pipeline(pl, SPAN, NG, DOWN_LAG, step)

        @block.vector
        def _(dve):
            v = nc.vector

            def mask_up(g, e):
                if g.live():
                    dve.wait_ge(route_kept, g.count(ROUTE, 2 + e))
                    dve.wait_ge(lo_ready, g.count(1, 1))
                    dve.wait_ge(up_used, g.count(E, e - 1))
                    v.tensor_tensor(hm[e % 2][:, :, :], h_half[g.slot][:, :, :],
                                    masks[g.slot][:, e, :].unsqueeze(1).to_broadcast([P, 2, GT]), ALU.mult).then_inc(masked, 1)

            def mask_down(g, e):
                if g.live():
                    dve.wait_ge(h1_lo, g.count(2 * FB, 2 * FB))
                    for f in range(FB):
                        k = FB * e + f
                        dve.wait_ge(down_used, g.count(FB * E, max(k - 3, 0)))
                        v.tensor_tensor(h1m[k % 4][:, :, :], h1[g.slot][:, :, f, :],
                                        masks[g.slot][:, e, :].unsqueeze(1).to_broadcast([P, 2, GT]), ALU.mult).then_inc(h1_masked, 1)

            def route(g, part):
                if not g.live():
                    return

                def done(k, ins):
                    ins.then_inc(router, 1)

                def after(k):
                    dve.wait_ge(router, g.count(7, k))

                if part == 0:
                    dve.wait_ge(head_kept, g.count(2, 2))
                    done(1, v.tensor_reduce(top[:, 0, :], logits[:, :, :], AX.X, ALU.max))
                    after(1)
                    done(2, v.tensor_tensor(below[:, :, :], logits[:, :, :], top[:, 0, :].unsqueeze(2).to_broadcast([P, GB, E]),
                                            ALU.subtract))
                    after(2)
                    done(3, v.scalar_tensor_tensor(cand[:, :, :], below[:, :, :], 0.0,
                                                   m.rank[:, :].unsqueeze(1).to_broadcast([P, GB, E]), ALU.is_ge, ALU.mult))
                    after(3)
                    done(4, v.tensor_reduce(top[:, 1, :], cand[:, :, :], AX.X, ALU.max))
                else:
                    after(4)
                    dve.wait_ge(route_tile, g.count(ROUTE, 1 - ROUTE))
                    done(5, v.tensor_tensor(choice[:, :, 0:E], cand[:, :, :], top[:, 1, :].unsqueeze(2).to_broadcast([P, GB, E]),
                                            ALU.is_equal))
                    dve.wait_ge(exped, g.count(1, 1))
                    done(6, v.tensor_reduce(top[:, 2, :], ex[:, :, :], AX.X, ALU.add))
                    after(6)
                    done(7, v.reciprocal(top[:, 2, :], top[:, 2, :]))
                    after(7)
                    v.tensor_tensor(choice[:, :, E:], choice[:, :, 0:E], top[:, 2, :].unsqueeze(2).to_broadcast([P, GB, E]),
                                    ALU.mult).then_inc(onehot, 1)

            def gate(g, k):
                if g.live():
                    f = GATED[k]
                    dve.wait_ge(tanhed, g.count(2 * FB, k + 1))
                    v.scalar_tensor_tensor(th[:, f, :], th[:, f, :], 1.0, z[:, f, :], ALU.add, ALU.mult).then_inc(gated, 1)

            def step(t):
                up, down = t.back(UP_LAG), t.back(DOWN_LAG)
                head = t.live()
                rows = group_rows(m, t)
                if head:
                    norm_stats(nc, dve, norm, t, rows)
                for e in range(E // 2):
                    mask_up(up, 2 * e)
                    mask_up(up, 2 * e + 1)
                    mask_down(down, e)
                    if head and e == 1:
                        dve.wait_ge(head_tile, t.count(2, -1))
                        norm_apply(nc, dve, norm, t, rows, lambda b: hn[:, b, :])
                mask_down(down, 4)
                if up.live():
                    dve.wait_ge(up_used, up.count(E, E))
                    dve.wait_ge(route_kept, up.count(ROUTE, 11))
                    dve.wait_ge(tanhed, up.count(2 * FB))
                    for f in range(FB):
                        v.tensor_tensor(z[:, f, :], up_bank[f][:, :], s1_tok[:, f, :], ALU.mult).then_inc(z_scaled, 1)
                mask_down(down, 5)
                mask_down(down, 6)
                gate(up, 2)
                gate(up, 3)
                route(t, 0)
                mask_down(down, 7)
                route(t, 1)
                if down.live():
                    dve.wait_ge(down_used, down.count(FB * E, FB * E))
                    dve.wait_ge(route_kept, down.count(ROUTE, 12))
                    v.tensor_tensor(routed[:, :], down_bank[0][:, :], s2_tok[down.slot][:, :], ALU.mult).then_inc(y_step, 1)
                    dve.wait_ge(y_step, down.count(1, 1))
                    dve.wait_ge(y_turned, down.count(1))
                    v.scalar_tensor_tensor(y[:, :], down_bank[1][:, :], m.s2_own[:, 0:1], routed[:, :], ALU.mult, ALU.add
                                           ).then_inc(y_ready, 1)
                if down.live():
                    dve.wait_ge(y_turned, down.count(1, 1))
                    xg = m.x[:, bass.ds(down.count(GB), GB), :].rearrange("p b d -> p (b d)")
                    v.tensor_tensor(xg, down_bank[0][:, :], xg, ALU.add).then_inc(added, 1)

            pipeline(dve, SPAN, NG, DOWN_LAG, step)

        @block.scalar
        def _(act):
            f_ = nc.scalar

            def kept(g, k):
                act.wait_ge(route_tile, g.count(ROUTE, k + 1))

            def tanh(g, k):
                f = GATED[k]
                f_.activation(th[:, f, :], z[:, f, :], ACT.Tanh, scale=1.0 / SPLIT).then_inc(tanhed, 1)

            def upper(g, k):
                f = GATED[k]
                if k < FB:
                    act.wait_ge(gate_step, g.count(2 * FB, 2 * k + 2))
                else:
                    act.wait_ge(gated, g.count(FB, k - FB + 1))
                f_.activation(h1[g.slot][:, 0, f, :], th[:, f, :], ACT.Copy).then_inc(h1_hi, 1)

            def step(t):
                up = t.back(UP_LAG)
                if up.live():
                    act.wait_ge(h1_masked, up.count(FB * E, -FB * E))
                    for e in range(E):
                        kept(up, 1 + e)
                        f_.activation(masks[up.slot][:, e, :], front_bank[(1 + e) % 2][:, :], ACT.Copy).then_inc(route_kept, 1)
                    act.wait_ge(up_used, up.count(E, 1))
                    act.wait_ge(gated, up.count(FB))
                    act.wait_ge(gate_step, up.count(2 * FB))
                    for f in range(FB):
                        f_.activation(z[:, FB + f, :], up_bank[FB + f][:, :], ACT.Identity, scale=m.s1_own[:, f:f + 1]
                                      ).then_inc(z_own, 1)
                    act.wait_ge(z_own, up.count(FB, FB))
                    act.wait_ge(h1_lo, up.count(2 * FB))
                    act.wait_ge(z_scaled, up.count(FB))
                    for f in range(FB):
                        kept(up, 9 + f)
                        f_.activation(s1_tok[:, f, :], front_bank[(9 + f) % 2][:, :], ACT.Copy).then_inc(route_kept, 1)
                    tanh(up, 0)
                    tanh(up, 1)
                    kept(up, 11)
                    act.wait_ge(y_step, up.count(1, -1))
                    f_.activation(s2_tok[up.slot][:, :], front_bank[1][:, :], ACT.Copy).then_inc(route_kept, 1)
                    act.wait_ge(down_used, up.count(FB * E, -FB * E))
                if t.live():
                    act.wait_ge(head_tile, t.count(2, 1))
                    act.wait_ge(lo_ready, t.count(1))
                    act.wait_ge(up_used, t.count(E, -E))
                    for dst in (h_t[:, :], h_half[t.slot][:, 0, :]):
                        last = f_.activation(dst, front_bank[0][:, :], ACT.Identity, scale=m.gb[:, 0:1], bias=m.gb[:, 1:2])
                    last.then_inc(head_kept, 1)
                if up.live():
                    act.wait_ge(z_scaled, up.count(FB, FB))
                    tanh(up, 2)
                    tanh(up, 3)
                if t.live():
                    act.wait_ge(head_tile, t.count(2, 2))
                    f_.activation(logits[:, :, :].rearrange("p b e -> p (b e)"), front_bank[1][:, 0:GB * E], ACT.Copy
                                  ).then_inc(head_kept, 1)
                    act.wait_ge(router, t.count(7, 2))
                    f_.activation(ex[:, :, :].rearrange("p b e -> p (b e)"), below[:, :, :].rearrange("p b e -> p (b e)"),
                                  ACT.Exp, scale=1.0 / SPLIT).then_inc(exped, 1)
                if up.live():
                    upper(up, 0)
                    upper(up, 1)
                    upper(up, 2)
                    upper(up, 3)
                if t.live():
                    kept(t, 0)
                    f_.activation(m.o_t32[0:2 * E, :], front_bank[0][0:2 * E, :], ACT.Copy)
                    f_.activation(m.o_t16[0:2 * E, :], front_bank[0][0:2 * E, :], ACT.Copy).then_inc(route_kept, 1)

            pipeline(act, SPAN, NG, DOWN_LAG, step)

        @block.tensor
        def _(pe):
            mm = nc.tensor

            def tile(g, k):
                if k >= 2:
                    pe.wait_ge(route_kept, g.count(ROUTE, k - 1))
                return front_bank[k % 2]

            def mask(g, e):
                if g.live():
                    mm.matmul(tile(g, 1 + e)[:, :], m.pick[:, e, :], m.o_t16[:, :], start=True, stop=True).then_inc(route_tile, 1)

            def project_up(g, e):
                if g.live():
                    pe.wait_ge(masked, g.count(E, e + 1))
                    for f in range(FB):
                        for part in range(2):
                            last = mm.matmul(up_bank[f][:, :], m.w_t[:, W1E + FB * e + f, :], hm[e % 2][:, part, :],
                                             start=e + part == 0, stop=e + part == E)
                    last.then_inc(up_used, 1)

            def project_down(g, e):
                if g.live():
                    for f in range(FB):
                        k = FB * e + f
                        pe.wait_ge(h1_masked, g.count(FB * E, k + 1))
                        for part in range(2):
                            last = mm.matmul(down_bank[0][:, :], m.w_t[:, W2E + k, :], h1m[k % 4][:, part, :],
                                             start=k + part == 0, stop=k + part == FB * E)
                        last.then_inc(down_used, 1)

            def step(t):
                up, down = t.back(UP_LAG), t.back(DOWN_LAG)
                if up.live():
                    pe.wait_ge(route_kept, up.count(ROUTE, 1))
                mask(up, 0)
                mask(up, 1)
                if up.live():
                    pe.wait_ge(lo_ready, up.count(1, 1))
                    pe.wait_ge(z_scaled, up.count(FB))
                    pe.wait_ge(z_own, up.count(FB))
                    for f in range(FB):
                        for part in range(2):
                            mm.matmul(up_bank[FB + f][:, :], m.w_t[:, W1S + f, :], h_half[up.slot][:, part, :],
                                      start=part == 0, stop=part == 1)
                if down.live():
                    pe.wait_ge(h1_lo, down.count(2 * FB, FB))
                    pe.wait_ge(y_ready, down.count(1))
                    for f in range(FB):
                        for part in range(2):
                            mm.matmul(down_bank[1][:, :], m.w_t[:, W2S + f, :], h1[down.slot][:, part, FB + f, :],
                                      start=f + part == 0, stop=f + part == 2)
                    pe.wait_ge(added, down.count(1))
                mask(up, 2)
                mask(up, 3)
                for e in range(E // 2):
                    project_up(up, 2 * e)
                    if e < 2:
                        mask(up, 4 + 2 * e)
                    project_up(up, 2 * e + 1)
                    if e < 2:
                        mask(up, 5 + 2 * e)
                    if e == 2 and up.live():
                        for f in range(FB):
                            mm.matmul(tile(up, 9 + f)[:, :], m.s1_t[:, f, :], m.o_t32[:, :], start=True, stop=True).then_inc(route_tile, 1)
                    project_down(down, e)
                if up.live():
                    mm.matmul(tile(up, 11)[:, :], m.s2_t[:, :], m.o_t32[:, :], start=True, stop=True).then_inc(route_tile, 1)
                if t.live():
                    pe.wait_ge(norm.normed, t.count(1, 1))
                    pe.wait_ge(route_kept, t.count(ROUTE, -1))
                    for b in range(GB):
                        last = mm.transpose(front_bank[0][:, S * b:S * b + S], hn[:, b, :], m.id32[:, :])
                    last.then_inc(head_tile, 1)
                project_down(down, 4)
                if t.live():
                    pe.wait_ge(head_kept, t.count(2, 1))
                    pe.wait_ge(route_kept, t.count(ROUTE))
                    for b in range(GB):
                        last = mm.matmul(front_bank[1][:, E * b:E * b + E], h_t[:, S * b:S * b + S], m.rw[:, :], start=True, stop=True)
                    last.then_inc(head_tile, 1)
                for e in range(5, E):
                    project_down(down, e)
                if t.live():
                    pe.wait_ge(onehot, t.count(1, 1))
                    pe.wait_ge(head_kept, t.count(2, 2))
                    for b in range(GB):
                        last = mm.transpose(tile(t, 0)[0:2 * E, S * b:S * b + S], choice[:, b, :], m.id32[:, :])
                    last.then_inc(route_tile, 1)
                if down.live():
                    pe.wait_ge(y_step, down.count(1, 1))
                    pe.wait_ge(y_ready, down.count(1, 1))
                    for b in range(GB):
                        last = mm.transpose(down_bank[0][:, S * b:S * b + S], y[:, S * b:S * b + S], m.id32[:, :])
                    last.then_inc(y_turned, 1)

            pipeline(pe, SPAN, NG, DOWN_LAG, step)


def conv_ffn(nc, m, a, sem, out):
    UP_LAG, DOWN_LAG, SPAN = 1, 2, 2
    n = "c_"

    def s(name):
        return sem(n + name)

    quant, scaled_up, head_clipped, by_token, cleared = s("quant"), s("scaled_up"), s("head_clipped"), s("by_token"), s("cleared")
    q_turned, q_kept, r_spread, r_kept = s("q_turned"), s("q_kept"), s("r_spread"), s("r_kept")
    uped, scaled, centred, left, right, tanhed = (s(x) for x in ("uped", "scaled", "centred", "left", "right", "tanhed"))
    hidden_dve, hidden_pool = s("hidden_dve"), s("hidden_pool")
    h_turned, requant, quantised, clipped, h_levels = s("h_turned"), s("requant"), s("quantised"), s("clipped"), s("h_levels")
    l_turned, l_kept, downed, added, stored = s("l_turned"), s("l_kept"), s("downed"), s("added"), s("stored")

    with ExitStack() as st:
        def sb(name, shape, dt=F32):
            return st.enter_context(nc.sbuf_tensor(n + name, shape, dt))

        norm = Norm(nc, st, sem, n)
        xn = sb("xn", [P, GB, D])
        amax = sb("amax", [P, 3, GB])
        back = [sb(f"back{i}", [P, GB]) for i in range(2)]
        whole = sb("whole", [P, GB, D])
        lev = sb("lev", [P, GB, D], F16)
        lev_t = sb("lev_t", [P, GT], F16)
        r_tok = sb("r_tok", [P, GT])
        zp = sb("zp", [P, CB, GB, S + 2])
        yc = sb("yc", [P, CB, GT])
        th = sb("th", [P, CB, GT])
        hid = [sb(f"hid{i}", [P, CB, GT]) for i in range(2)]
        amax2 = [sb(f"amax2_{i}", [P, 4]) for i in range(GB)]
        whole2 = [sb(f"whole2_{i}", [P, CF]) for i in range(2)]
        lev2 = [sb(f"lev2_{i}", [P, CF], F16) for i in range(2)]
        lev2_t = [sb(f"lev2_t{i}", [P, CB, S], F16) for i in range(2)]
        block = st.enter_context(nc.Block())

        up_bank, hid_bank, level_bank, head_bank, down_bank = m.bank[0:2], m.bank[2:4], m.bank[4:6], m.bank[6], m.bank[7]

        @block.sync
        def _(sp):
            def step(t):
                g = t.back(DOWN_LAG)
                if g.live():
                    sp.wait_ge(added, g.count(GB, GB))
                    sp.dma_start(out[bass.ds(g.count(GB), GB), :, :].rearrange("b p d -> p b d"),
                                 m.x[:, bass.ds(g.count(GB), GB), :]).then_inc(stored, 16)

            pipeline(sp, SPAN, NG, DOWN_LAG, step)
            sp.wait_ge(stored, 16 * NG)

        @block.gpsimd
        def _(pl):
            gp = nc.gpsimd

            def gate(g, k):
                if g.live():
                    out, done = hid[g.slot][:, k, :], g.count(2 * (CB - 1), 2 * k + 1)
                    pl.wait_ge(h_turned, g.count(GB, -GB))
                    pl.wait_ge(tanhed, g.count(CB, k + 1))
                    gp.tensor_tensor(out=out, in0=th[:, k, :], in1=yc[:, k, :], op=ALU.mult).then_inc(hidden_pool, 1)
                    pl.wait_ge(hidden_pool, done)
                    gp.tensor_tensor(out=out, in0=out, in1=yc[:, k, :], op=ALU.add).then_inc(hidden_pool, 1)

            def step(t):
                up = t.back(UP_LAG)
                if t.live():
                    norm_rstd(nc, m, pl, norm, t)
                for k in range(CB - 1):
                    gate(up, k)

            pipeline(pl, SPAN, NG, DOWN_LAG, step)

        @block.vector
        def _(dve):
            v = nc.vector

            def head_scale(g):
                dve.wait_ge(norm.normed, g.count(1, 1))

                def after(k):
                    dve.wait_ge(quant, g.count(5, k))

                v.tensor_reduce(amax[:, 0, :], xn[:, :, :], AX.X, ALU.max, apply_absolute_value=True).then_inc(quant, 1)
                after(1)
                v.tensor_scalar(amax[:, 1, :], amax[:, 0, :], EPS, None, ALU.max).then_inc(quant, 1)
                after(2)
                dve.wait_ge(scaled_up, g.count(1))
                v.reciprocal(amax[:, 2, :], amax[:, 1, :]).then_inc(quant, 1)
                dve.wait_ge(r_spread, g.count(1, -1))
                v.tensor_scalar(back[g.slot][:, :], amax[:, 1, :], m.sc[:, 0:1], 1.0 / 127.0, ALU.mult, ALU.mult).then_inc(quant, 1)
                after(3)
                v.tensor_scalar(amax[:, 2, :], amax[:, 2, :], 127.0, None, ALU.mult).then_inc(quant, 1)

            def hidden_scale(g, b, part):
                if not g.live():
                    return
                am = amax2[b]
                if part == 0:
                    dve.wait_ge(h_turned, g.count(GB, b + 1))
                    v.tensor_reduce(am[:, 0:1], hid_bank[b % 2][:, :], AX.X, ALU.max, apply_absolute_value=True).then_inc(requant, 1)
                if part == 1:
                    dve.wait_ge(requant, g.count(5 * GB, 5 * b + 1))
                    v.tensor_scalar(am[:, 1:2], am[:, 0:1], EPS, None, ALU.max).then_inc(requant, 1)
                if part == 2:
                    dve.wait_ge(requant, g.count(5 * GB, 5 * b + 2))
                    v.reciprocal(am[:, 2:3], am[:, 1:2]).then_inc(requant, 1)
                    v.tensor_scalar(am[:, 3:4], am[:, 1:2], m.sc[:, 1:2], 1.0 / 127.0, ALU.mult, ALU.mult).then_inc(requant, 1)
                if part == 3:
                    dve.wait_ge(requant, g.count(5 * GB, 5 * b + 3))
                    v.tensor_scalar(am[:, 2:3], am[:, 2:3], 127.0, None, ALU.mult).then_inc(requant, 1)

            def head_clip(g):
                if g.live():
                    dve.wait_ge(scaled_up, g.count(1, 1))
                    v.tensor_scalar(whole[:, :, :], whole[:, :, :], ROUND + 127.0, ROUND - 128.0, ALU.min, ALU.max
                                    ).then_inc(head_clipped, 1)

            def hidden_clip(g, b):
                if g.live():
                    dve.wait_ge(quantised, g.count(GB, b + 1))
                    v.tensor_scalar(whole2[b % 2][:, :], whole2[b % 2][:, :], ROUND + 127.0, ROUND - 128.0, ALU.min, ALU.max
                                    ).then_inc(clipped, 1)

            def left_tap(g, k):
                if g.live():
                    y3 = yc[:, k, :].rearrange("p (b s) -> p b s", b=GB)
                    dve.wait_ge(centred, g.count(CB, k + 1))
                    v.scalar_tensor_tensor(y3, zp[:, k, :, 0:S], m.cw[:, k, 0:1], y3, ALU.mult, ALU.add).then_inc(left, 1)

            def right_tap(g, k):
                if g.live():
                    y3 = yc[:, k, :].rearrange("p (b s) -> p b s", b=GB)
                    dve.wait_ge(left, g.count(CB, k + 1))
                    v.scalar_tensor_tensor(y3, zp[:, k, :, 2:S + 2], m.cw[:, k, 2:3], y3, ALU.mult, ALU.add).then_inc(right, 1)

            def gate(g, k):
                if g.live():
                    dve.wait_ge(tanhed, g.count(CB, k + 1))
                    dve.wait_ge(h_turned, g.count(GB, -GB))
                    v.scalar_tensor_tensor(hid[g.slot][:, k, :], th[:, k, :], 1.0, yc[:, k, :], ALU.add, ALU.mult
                                           ).then_inc(hidden_dve, 1)

            def down_add(g, b):
                if g.live():
                    dve.wait_ge(downed, g.count(GB, b + 1))
                    xb = m.x[:, bass.ds(g.count(GB, b), 1), :].rearrange("p b d -> p (b d)")
                    v.scalar_tensor_tensor(xb, down_bank[:, 0:D], amax2[b][:, 3:4], xb, ALU.mult, ALU.add).then_inc(added, 1)

            def step(t):
                up, down = t.back(UP_LAG), t.back(DOWN_LAG)
                rows = group_rows(m, t)
                if t.live():
                    norm_stats(nc, dve, norm, t, rows)
                for k in range(CB):
                    if up.live():
                        dve.wait_ge(uped, up.count(CB, k + 1))
                        dve.wait_ge(r_kept, up.count(1, 1))
                        dve.wait_ge(centred, up.count(CB, k - CB + 1))
                        v.tensor_tensor(zp[:, k, :, 1:S + 1], up_bank[k % 2][:, :].rearrange("p (b s) -> p b s", b=GB),
                                        r_tok[:, :].rearrange("p (b s) -> p b s", b=GB), ALU.mult).then_inc(scaled, 1)
                    hidden_scale(down, k, 0)
                    hidden_scale(down, k, 1)
                    if k >= 1:
                        hidden_clip(down, k - 1)
                        left_tap(up, k - 1)
                    hidden_scale(down, k, 2)
                    if k >= 1:
                        right_tap(up, k - 1)
                    hidden_scale(down, k, 3)
                    if k == 3:
                        down_add(down, 0)
                        head_clip(t)
                    if k == 1 and t.live():
                        dve.wait_ge(scaled_up, t.count(1))
                        norm_apply(nc, dve, norm, t, rows, lambda b: xn[:, b, :])
                    if k == 2 and t.live():
                        head_scale(t)
                left_tap(up, CB - 1)
                down_add(down, 1)
                hidden_clip(down, GB - 1)
                right_tap(up, CB - 1)
                down_add(down, 2)
                gate(up, CB - 1)
                down_add(down, 3)

            v.memset(zp[:, :, :, :].rearrange("p c b s -> p (c b s)"), 0.0).then_inc(cleared, 1)
            dve.wait_ge(cleared, 1)
            pipeline(dve, SPAN, NG, DOWN_LAG, step)

        @block.scalar
        def _(act):
            f_ = nc.scalar

            def centre(g, k):
                if g.live():
                    act.wait_ge(scaled, g.count(CB, k + 1))
                    act.wait_ge(hidden_dve, g.count(1))
                    act.wait_ge(hidden_pool, g.count(2 * (CB - 1)))
                    f_.activation(yc[:, k, :].rearrange("p (b s) -> p b s", b=GB), zp[:, k, :, 1:S + 1], ACT.Identity,
                                  scale=m.cw[:, k, 1:2], bias=m.cb[:, k:k + 1]).then_inc(centred, 1)

            def tanh(g, k):
                if g.live():
                    act.wait_ge(right, g.count(CB, k + 1))
                    f_.activation(th[:, k, :], yc[:, k, :], ACT.Tanh).then_inc(tanhed, 1)

            def quantise(g, b):
                if g.live():
                    act.wait_ge(requant, g.count(5 * GB, 5 * b + 5))
                    f_.activation(whole2[b % 2][:, :], hid_bank[b % 2][:, :], ACT.Identity, scale=amax2[b][:, 2:3], bias=m.round[:, 0:1]
                                  ).then_inc(quantised, 1)

            def to_levels(g, b):
                if g.live():
                    act.wait_ge(clipped, g.count(GB, b + 1))
                    act.wait_ge(l_turned, g.count(GB, max(b - 1, 0)))
                    f_.activation(lev2[b % 2][:, :], whole2[b % 2][:, :], ACT.Copy, bias=-ROUND).then_inc(h_levels, 1)

            def keep_levels(g, b):
                if g.live():
                    act.wait_ge(l_turned, g.count(GB, b + 1))
                    act.wait_ge(downed, g.count(GB, max(b - 1, 0)))
                    f_.activation(lev2_t[b % 2][:, :, :].rearrange("p c s -> p (c s)"), level_bank[b % 2][:, 0:256].bitcast(F16),
                                  ACT.Copy).then_inc(l_kept, 1)

            def step(t):
                up, down = t.back(UP_LAG), t.back(DOWN_LAG)
                for k in range(CB):
                    if k >= 1:
                        to_levels(down, k - 1)
                    centre(up, k)
                    quantise(down, k)
                    if k >= 1:
                        keep_levels(down, k - 1)
                    if k >= 2:
                        tanh(up, k - 2)
                    if k == 2 and t.live():
                        act.wait_ge(quant, t.count(5, 5))
                        for b in range(GB):
                            last = f_.activation(whole[:, b, :], xn[:, b, :], ACT.Identity, scale=amax[:, 2, b:b + 1], bias=m.round[:, 0:1])
                        last.then_inc(scaled_up, 1)
                if t.live():
                    act.wait_ge(head_clipped, t.count(1, 1))
                    act.wait_ge(q_turned, t.count(1))
                    f_.activation(lev[:, :, :].rearrange("p b d -> p (b d)"), whole[:, :, :].rearrange("p b d -> p (b d)"),
                                  ACT.Copy, bias=-ROUND).then_inc(by_token, 1)
                to_levels(down, GB - 1)
                if t.live():
                    act.wait_ge(q_turned, t.count(1, 1))
                    act.wait_ge(uped, t.count(CB))
                    f_.activation(lev_t[:, :], head_bank[:, 0:256].bitcast(F16), ACT.Copy).then_inc(q_kept, 1)
                tanh(up, CB - 2)
                keep_levels(down, GB - 1)
                tanh(up, CB - 1)
                if t.live():
                    act.wait_ge(r_spread, t.count(1, 1))
                    act.wait_ge(scaled, t.count(CB))
                    f_.activation(r_tok[:, :], head_bank[:, :], ACT.Copy).then_inc(r_kept, 1)

            pipeline(act, SPAN, NG, DOWN_LAG, step)

        @block.tensor
        def _(pe):
            mm = nc.tensor

            def turn_hidden(g, b):
                if g.live():
                    pe.wait_ge(quantised, g.count(GB, max(b - 1, 0)))
                    for k in range(CB):
                        last = mm.transpose(hid_bank[b % 2][:, P * k:P * k + P], hid[g.slot][:, k, S * b:S * b + S], m.id32[:, :])
                    last.then_inc(h_turned, 1)

            def turn_levels(g, b):
                if g.live():
                    pe.wait_ge(h_levels, g.count(GB, b + 1))
                    pe.wait_ge(l_kept, g.count(GB, max(b - 1, 0)))
                    for k in range(CB):
                        last = mm.transpose(level_bank[b % 2][:, 64 * k:64 * k + 64].bitcast(F16), lev2[b % 2][:, P * k:P * k + P],
                                            m.id16[:, :])
                    last.then_inc(l_turned, 1)

            def project_down(g, b):
                if g.live():
                    pe.wait_ge(l_kept, g.count(GB, b + 1))
                    pe.wait_ge(added, g.count(GB, b))
                    for k in range(CB):
                        last = mm.matmul(down_bank[:, 0:D], lev2_t[b % 2][:, k, :], m.w_t[:, W2C + k, :], start=k == 0, stop=k == CB - 1)
                    last.then_inc(downed, 1)

            def step(t):
                up, down = t.back(UP_LAG), t.back(DOWN_LAG)
                for k in range(CB):
                    if up.live():
                        pe.wait_ge(q_kept, up.count(1, 1))
                        pe.wait_ge(scaled, up.count(CB, max(k - 1, 0)))
                        mm.matmul(up_bank[k % 2][:, :], m.w_t[:, W1C + k, :], lev_t[:, :], start=True, stop=True).then_inc(uped, 1)
                    if k == 0:
                        if down.live():
                            pe.wait_ge(hidden_dve, down.count(1, 1))
                            pe.wait_ge(hidden_pool, down.count(2 * (CB - 1), 2 * (CB - 1)))
                        turn_hidden(down, 0)
                        turn_hidden(down, 1)
                    if k >= 1:
                        turn_levels(down, k - 1)
                    if k in (1, 2):
                        turn_hidden(down, k + 1)
                    if k >= 2:
                        project_down(down, k - 2)
                project_down(down, GB - 2)
                if t.live():
                    pe.wait_ge(by_token, t.count(1, 1))
                    pe.wait_ge(r_kept, t.count(1))
                    for b in range(GB):
                        last = mm.transpose(head_bank[:, 64 * b:64 * b + 64].bitcast(F16), lev[:, b, :], m.id16[:, :])
                    last.then_inc(q_turned, 1)
                turn_levels(down, GB - 1)
                if t.live():
                    pe.wait_ge(q_kept, t.count(1, 1))
                    for b in range(GB):
                        last = mm.matmul(head_bank[:, S * b:S * b + S], back[t.slot][:, b:b + 1].to_broadcast([P, P]), m.id32[:, :],
                                         start=True, stop=True)
                    last.then_inc(r_spread, 1)
                project_down(down, GB - 1)

            pipeline(pe, SPAN, NG, DOWN_LAG, step)


def program(nc, a, out):
    with ExitStack() as st:
        def sem(name):
            return st.enter_context(nc.semaphore(name))

        def sb(name, shape, dt=F32):
            return st.enter_context(nc.sbuf_tensor(name, shape, dt))

        m = Memory()
        m.bank = [st.enter_context(nc.psum_tensor(f"bank{i}", [P, 512], F32)) for i in range(8)]
        m.x = sb("x_res", [P, B, D])
        m.x_in = sem("x_in")
        m.wq = [sb("wq0", [D, D]), sb("wq1", [D, D])]
        m.wk = [sb("wk0", [D, DH]), sb("wk1", [D, D])]
        m.wv = [sb("wv0", [D, DH]), sb("wv1", [D, D])]
        m.wo = [sb("wo0", [D, D]), sb("wo1", [D, D])]
        m.qkb, m.bv, m.bo = sb("qkb", [D, 2]), sb("bv", [D, 1]), sb("bo", [P, D])
        m.rw, m.gb = sb("rw", [D, E]), sb("gb", [D, 2])
        m.cw, m.cb = sb("cw", [P, CB, 3]), sb("cb", [P, CB])
        m.w_t = sb("w_t", [P, NW, P], F16)
        m.s1, m.s2, m.sc = sb("s1", [P, (E + 1) * FB]), sb("s2", [P, E + 1]), sb("sc", [P, 2])
        m.s1_own, m.s2_own = sb("s1_own", [P, FB]), sb("s2_own", [P, 1])
        m.s1_t, m.s2_t = sb("s1_t", [P, FB, P]), sb("s2_t", [P, P])
        m.o_t32, m.o_t16 = sb("o_t32", [P, GT]), sb("o_t16", [P, GT], F16)
        m.id32, m.id16, m.ones = sb("id32", [P, P]), sb("id16", [P, P], F16), sb("ones", [P, P])
        m.minus_half, m.quarter, m.per_d, m.eps = (sb(x, [P, GB]) for x in ("minus_half", "quarter", "per_d", "eps"))
        m.rank, m.round = sb("rank", [P, E]), sb("round", [P, 1])
        m.gather, m.shift = sb("gather", [P, 4, VW]), sb("shift", [P, 2])
        m.pick = sb("pick", [P, E, P], F16)
        m.band_q, m.band_k, m.plain_k = sb("band_q", [P, 2, S // 2], F16), sb("band_k", [P, 2, S], F16), sb("plain_k", [P, S], F16)

        setup(nc, m, a, sem)
        attention(nc, m, a, sem, 0)
        expert_ffn(nc, m, a, sem)
        attention(nc, m, a, sem, 1)
        conv_ffn(nc, m, a, sem, out)


def laid_out(inputs):
    import numpy as np

    by_dim = np.arange(D).reshape(H, DH).T.reshape(-1)
    by_turn = np.arange(D).reshape(4, H // 4, DH).transpose(1, 0, 2).reshape(-1)
    get = {k: np.asarray(v) for k, v in inputs.items()}
    wkv = get["L0_xattn_w_kv"]
    arrays = {
        "x": get["x"], "ctx": get["ctx_1024"],
        "wq0": get["L0_xattn_w_q"][:, by_dim], "wk0": wkv[:, :DH], "wv0": wkv[:, DH:], "wo0": get["L0_xattn_w_o"][by_turn],
        "wq1": get["L1_xattn_Wq"].T[:, by_dim], "wk1": get["L1_xattn_Wk"].T[:, by_dim],
        "wv1": get["L1_xattn_Wv"].T, "wo1": get["L1_xattn_Wo"].T[by_turn],
        "bqk": np.stack([get["L1_xattn_bq"][by_dim], get["L1_xattn_bk"][by_dim]], 1),
        "bv": get["L1_xattn_bv"][by_turn][:, None], "bo": get["L1_xattn_bo"][None, :],
        "w1s": get["L0_ffn_shared_w1"], "w2s": get["L0_ffn_shared_w2"],
        "w1e": get["L0_ffn_expert_w1"], "w2e": get["L0_ffn_expert_w2"],
        "rw": get["L0_ffn_router_w"].T, "gb": np.stack([get["L0_ffn_ln_gamma"], get["L0_ffn_ln_beta"]], 1),
        "w1c": get["L1_ffn_w1"], "w2c": get["L1_ffn_w2"],
        "cw": get["L1_ffn_conv_w"].reshape(CB, P, 3).transpose(1, 0, 2), "cb": get["L1_ffn_conv_b"].reshape(CB, P).T,
    }
    return {k: np.ascontiguousarray(v) for k, v in arrays.items()}


def kernel(**inputs):
    import concourse.bacc as bacc
    from concourse.bass_utils import run_bass_kernel_spmd

    arrays = laid_out(inputs)
    nc = bacc.Bacc("TRN2", target_bir_lowering=False, num_devices=1)
    a = {k: nc.dram_tensor(f"in_{k}", v.shape, mybir.dt.from_np(v.dtype), kind="ExternalInput").ap() for k, v in arrays.items()}
    out = nc.dram_tensor("out_x", (B, S, D), F32, kind="ExternalOutput").ap()
    program(nc, a, out)
    r = run_bass_kernel_spmd(nc, [{f"in_{k}": v for k, v in arrays.items()}], core_ids=[0])
    return r.results[0]["out_x"]
```
